# Optimizing a Trainium2 kernel written in Bass

```python
import numpy as np
import jax
import jax.numpy as jnp

def _softmax(x, axis=-1):
    return jax.nn.softmax(x, axis=axis)

def _gelu(x):
    return jax.nn.gelu(x, approximate=True)

def _silu(x):
    return jax.nn.silu(x)

def _sigmoid(x):
    return jax.nn.sigmoid(x)

def _layernorm(x, axis=-1, eps=1e-05):
    m = jnp.mean(x, axis=axis, keepdims=True)
    v = jnp.var(x, axis=axis, keepdims=True)
    return (x - m) / jnp.sqrt(v + eps)

def _scatter_add(tgt, idx, src, axis=0):
    return tgt.at[idx].add(src)

def _segment_sum(src, seg, n):
    return jax.ops.segment_sum(src, seg, n)
kernel_name = 'mk_rec_standalone_d1_rec_r8_685a24'

def setup_inputs(seed: int=0):
    np.random.seed(seed)
    _w = jnp.asarray

    def _rec_inputs():
        import jax
        import jax.numpy as jnp
        _rk = jax.random.key(seed)
        r_dense_x = 8.7408e-05 + 1.0001 * jax.random.normal(jax.random.fold_in(_rk, 1), (512, 13), jnp.float32)
        r_lS_i = jnp.stack([jax.random.randint(jax.random.fold_in(jax.random.fold_in(_rk, 2), 0), (512,), 4, 99994, jnp.int32), jax.random.randint(jax.random.fold_in(jax.random.fold_in(_rk, 2), 1), (512,), 0, 99999, jnp.int32), jax.random.randint(jax.random.fold_in(jax.random.fold_in(_rk, 2), 2), (512,), 1, 99998, jnp.int32), jax.random.randint(jax.random.fold_in(jax.random.fold_in(_rk, 2), 3), (512,), 2, 99995, jnp.int32), jax.random.randint(jax.random.fold_in(jax.random.fold_in(_rk, 2), 4), (512,), 0, 99999, jnp.int32), jax.random.randint(jax.random.fold_in(jax.random.fold_in(_rk, 2), 5), (512,), 4, 12500, jnp.int32), jax.random.randint(jax.random.fold_in(jax.random.fold_in(_rk, 2), 6), (512,), 0, 99999, jnp.int32), jax.random.randint(jax.random.fold_in(jax.random.fold_in(_rk, 2), 7), (512,), 0, 99993, jnp.int32), jax.random.randint(jax.random.fold_in(jax.random.fold_in(_rk, 2), 8), (512,), 2, 99998, jnp.int32), jax.random.randint(jax.random.fold_in(jax.random.fold_in(_rk, 2), 9), (512,), 2, 12500, jnp.int32), jax.random.randint(jax.random.fold_in(jax.random.fold_in(_rk, 2), 10), (512,), 2, 12500, jnp.int32), jax.random.randint(jax.random.fold_in(jax.random.fold_in(_rk, 2), 11), (512,), 2, 99998, jnp.int32), jax.random.randint(jax.random.fold_in(jax.random.fold_in(_rk, 2), 12), (512,), 1, 99995, jnp.int32), jax.random.randint(jax.random.fold_in(jax.random.fold_in(_rk, 2), 13), (512,), 5, 12500, jnp.int32), jax.random.randint(jax.random.fold_in(jax.random.fold_in(_rk, 2), 14), (512,), 8, 12500, jnp.int32), jax.random.randint(jax.random.fold_in(jax.random.fold_in(_rk, 2), 15), (512,), 0, 99999, jnp.int32), jax.random.randint(jax.random.fold_in(jax.random.fold_in(_rk, 2), 16), (512,), 9, 99999, jnp.int32), jax.random.randint(jax.random.fold_in(jax.random.fold_in(_rk, 2), 17), (512,), 2, 99998, jnp.int32), jax.random.randint(jax.random.fold_in(jax.random.fold_in(_rk, 2), 18), (512,), 3, 12500, jnp.int32), jax.random.randint(jax.random.fold_in(jax.random.fold_in(_rk, 2), 19), (512,), 6, 99997, jnp.int32), jax.random.randint(jax.random.fold_in(jax.random.fold_in(_rk, 2), 20), (512,), 5, 12500, jnp.int32), jax.random.randint(jax.random.fold_in(jax.random.fold_in(_rk, 2), 21), (512,), 0, 99999, jnp.int32), jax.random.randint(jax.random.fold_in(jax.random.fold_in(_rk, 2), 22), (512,), 1, 12500, jnp.int32), jax.random.randint(jax.random.fold_in(jax.random.fold_in(_rk, 2), 23), (512,), 4, 99999, jnp.int32), jax.random.randint(jax.random.fold_in(jax.random.fold_in(_rk, 2), 24), (512,), 0, 99997, jnp.int32), jax.random.randint(jax.random.fold_in(jax.random.fold_in(_rk, 2), 25), (512,), 3, 12500, jnp.int32)], axis=0)
        return (r_dense_x, r_lS_i)
    r_dense_x, r_lS_i = _rec_inputs()

    def _L0_rec_setup():
        import jax, jax.numpy as jnp
        import numpy as np
        B = 4096
        M = 128
        N_TAB = 26
        N_ROWS = 12500
        LN_BOT = [13, 512, 256, 128]
        LN_TOP = [479, 1024, 1024, 1]
        _LI, _LJ = np.tril_indices(N_TAB + 1, k=-1)

        def _mlp_params(key, ln):
            ws, bs = ([], [])
            for i in range(len(ln) - 1):
                n, m = (ln[i], ln[i + 1])
                key, k1, k2 = jax.random.split(key, 3)
                ws.append(jax.random.normal(k1, (m, n), jnp.float32) * np.sqrt(2.0 / (m + n)))
                bs.append(jax.random.normal(k2, (m,), jnp.float32) * np.sqrt(1.0 / m))
            return (ws, bs)

        def _forward(dense_x, lS_i, emb_W, bot_w0, bot_b0, bot_w1, bot_b1, bot_w2, bot_b2, top_w0, top_b0, top_w1, top_b1, top_w2, top_b2):
            x = jax.nn.relu(dense_x @ bot_w0.T + bot_b0)
            x = jax.nn.relu(x @ bot_w1.T + bot_b1)
            x = jax.nn.relu(x @ bot_w2.T + bot_b2)
            ly = jax.vmap(lambda W, idx: W[idx])(emb_W, lS_i)
            T = jnp.concatenate([x[:, None, :], jnp.transpose(ly, (1, 0, 2))], axis=1)
            Z = jnp.einsum('bid,bjd->bij', T, T)
            Zflat = Z[:, _LI, _LJ]
            R = jnp.concatenate([x, Zflat], axis=1)
            z = jax.nn.relu(R @ top_w0.T + top_b0)
            z = jax.nn.relu(z @ top_w1.T + top_b1)
            p = jax.nn.sigmoid(z @ top_w2.T + top_b2)
            return p
        key = jax.random.key(seed)
        kd, ki, ke, kb, kt = jax.random.split(key, 5)
        dense_x = jax.random.normal(kd, (B, LN_BOT[0]), jnp.float32)
        lS_i = jax.random.randint(ki, (N_TAB, B), 0, N_ROWS, dtype=jnp.int64)
        lS_o = jnp.tile(jnp.arange(B, dtype=jnp.int64), (N_TAB, 1))
        bound = np.sqrt(1.0 / N_ROWS)
        emb_W = jax.random.uniform(ke, (N_TAB, N_ROWS, M), jnp.float32, -bound, bound)
        bw, bb = _mlp_params(kb, LN_BOT)
        tw, tb = _mlp_params(kt, LN_TOP)
        return {'dense_x': dense_x, 'lS_i': lS_i, 'lS_o': lS_o, 'emb_W': emb_W, 'bot_w0': bw[0], 'bot_b0': bb[0], 'bot_w1': bw[1], 'bot_b1': bb[1], 'bot_w2': bw[2], 'bot_b2': bb[2], 'top_w0': tw[0], 'top_b0': tb[0], 'top_w1': tw[1], 'top_b1': tb[1], 'top_w2': tw[2], 'top_b2': tb[2]}
    _L0_rec_all = _L0_rec_setup()
    _L0_rec_in = {k: v for k, v in _L0_rec_all.items() if k in ('lS_o', 'emb_W', 'bot_w0', 'bot_b0', 'bot_w1', 'bot_b1', 'bot_w2', 'bot_b2', 'top_w0', 'top_b0', 'top_w1', 'top_b1', 'top_w2', 'top_b2')}
    del _L0_rec_all
    return {'r_dense_x': r_dense_x, 'r_lS_i': r_lS_i, 'L0_rec_lS_o': _L0_rec_in['lS_o'], 'L0_rec_emb_W': _L0_rec_in['emb_W'], 'L0_rec_bot_w0': _L0_rec_in['bot_w0'], 'L0_rec_bot_b0': _L0_rec_in['bot_b0'], 'L0_rec_bot_w1': _L0_rec_in['bot_w1'], 'L0_rec_bot_b1': _L0_rec_in['bot_b1'], 'L0_rec_bot_w2': _L0_rec_in['bot_w2'], 'L0_rec_bot_b2': _L0_rec_in['bot_b2'], 'L0_rec_top_w0': _L0_rec_in['top_w0'], 'L0_rec_top_b0': _L0_rec_in['top_b0'], 'L0_rec_top_w1': _L0_rec_in['top_w1'], 'L0_rec_top_b1': _L0_rec_in['top_b1'], 'L0_rec_top_w2': _L0_rec_in['top_w2'], 'L0_rec_top_b2': _L0_rec_in['top_b2']}

def reference(r_dense_x, r_lS_i, L0_rec_lS_o, L0_rec_emb_W, L0_rec_bot_w0, L0_rec_bot_b0, L0_rec_bot_w1, L0_rec_bot_b1, L0_rec_bot_w2, L0_rec_bot_b2, L0_rec_top_w0, L0_rec_top_b0, L0_rec_top_w1, L0_rec_top_b1, L0_rec_top_w2, L0_rec_top_b2):
    import jax
    import jax.numpy as jnp

    def _L0_rec_ref(dense_x, lS_i, lS_o, emb_W, bot_w0, bot_b0, bot_w1, bot_b1, bot_w2, bot_b2, top_w0, top_b0, top_w1, top_b1, top_w2, top_b2):
        import jax, jax.numpy as jnp
        import numpy as np
        B = 4096
        M = 128
        N_TAB = 26
        N_ROWS = 12500
        LN_BOT = [13, 512, 256, 128]
        LN_TOP = [479, 1024, 1024, 1]
        _LI, _LJ = np.tril_indices(N_TAB + 1, k=-1)

        def _mlp_params(key, ln):
            ws, bs = ([], [])
            for i in range(len(ln) - 1):
                n, m = (ln[i], ln[i + 1])
                key, k1, k2 = jax.random.split(key, 3)
                ws.append(jax.random.normal(k1, (m, n), jnp.float32) * np.sqrt(2.0 / (m + n)))
                bs.append(jax.random.normal(k2, (m,), jnp.float32) * np.sqrt(1.0 / m))
            return (ws, bs)

        def _forward(dense_x, lS_i, emb_W, bot_w0, bot_b0, bot_w1, bot_b1, bot_w2, bot_b2, top_w0, top_b0, top_w1, top_b1, top_w2, top_b2):
            x = jax.nn.relu(dense_x @ bot_w0.T + bot_b0)
            x = jax.nn.relu(x @ bot_w1.T + bot_b1)
            x = jax.nn.relu(x @ bot_w2.T + bot_b2)
            ly = jax.vmap(lambda W, idx: W[idx])(emb_W, lS_i)
            T = jnp.concatenate([x[:, None, :], jnp.transpose(ly, (1, 0, 2))], axis=1)
            Z = jnp.einsum('bid,bjd->bij', T, T)
            Zflat = Z[:, _LI, _LJ]
            R = jnp.concatenate([x, Zflat], axis=1)
            z = jax.nn.relu(R @ top_w0.T + top_b0)
            z = jax.nn.relu(z @ top_w1.T + top_b1)
            p = jax.nn.sigmoid(z @ top_w2.T + top_b2)
            return p
        del lS_o
        return _forward(dense_x, lS_i, emb_W, bot_w0, bot_b0, bot_w1, bot_b1, bot_w2, bot_b2, top_w0, top_b0, top_w1, top_b1, top_w2, top_b2)
    y = _L0_rec_ref(r_dense_x, r_lS_i, L0_rec_lS_o, L0_rec_emb_W, L0_rec_bot_w0, L0_rec_bot_b0, L0_rec_bot_w1, L0_rec_bot_b1, L0_rec_bot_w2, L0_rec_bot_b2, L0_rec_top_w0, L0_rec_top_b0, L0_rec_top_w1, L0_rec_top_b1, L0_rec_top_w2, L0_rec_top_b2)
    return y

_drawn_inputs = setup_inputs


def setup_inputs(seed=0):
    import zlib

    import numpy as np

    out = dict(_drawn_inputs(seed))
    spreads = {}
    factors = {'r_dense_x': 8.0,
     'L0_rec_emb_W': 8.0,
     'L0_rec_bot_w0': 8.0,
     'L0_rec_bot_b0': 8.0,
     'L0_rec_bot_w1': 8.0,
     'L0_rec_bot_b1': 8.0,
     'L0_rec_bot_w2': 8.0,
     'L0_rec_bot_b2': 8.0,
     'L0_rec_top_w0': 6.238,
     'L0_rec_top_b0': 8.0,
     'L0_rec_top_w1': 8.0,
     'L0_rec_top_b1': 6.159,
     'L0_rec_top_w2': 7.959}
    for name, (base, spread) in spreads.items():
        noise = np.random.default_rng([zlib.crc32(name.encode()), seed]).standard_normal(out[name].shape)
        drawn = base * np.exp(spread * noise) if base else spread * noise
        out[name] = jnp.asarray(drawn.astype(out[name].dtype))
    for name, factor in factors.items():
        out[name] = (out[name] * factor).astype(out[name].dtype)
    return out
```

```python
from contextlib import ExitStack

import concourse.bass as bass
from concourse import mybir

F32 = mybir.dt.float32
F32R = mybir.dt.float32r
I32 = mybir.dt.int32
ACT = mybir.ActivationFunctionType
ALU = mybir.AluOpType

P = 128
B = 512
TILES = B // P
D = 128
TABLES = 26
ROWS = 12500
SLOTS = 32
NF = 1 + TABLES
S = P // SLOTS
G = P // S
PB = 4
ZBANKS = G // PB
NZ = S * TABLES
FC = 3
FK = NF // FC
COUNT = [FC * k + FC - 1 for k in range(FK)]
OFF = [sum(COUNT[:k]) for k in range(FK + 1)]
KZ = OFF[FK]
H = 1024
HC = H // P
N = 512
NH = H // N
DENSE, BOT0, BOT1 = 13, 512, 256
C0, C1 = BOT0 // P, BOT1 // P
GROUPS = [list(range(t, min(t + PB, TABLES))) for t in range(0, TABLES, PB)]
NG = len(GROUPS)
HALVES = [(0, 4), (4, NG)]
WCHUNKS = FC + HC


def program(nc, idx, dense_t, bot_w0_t, bot_b0, bot_w1_t, bot_b1, bot_w2_t, bot_b2,
            top_w0x_t, top_w0z_t, top_b0, top_w1_t, top_b1, top_w2, top_b2, emb, out):
    with ExitStack() as ctx:
        def sb(name, shape, dt=F32):
            return ctx.enter_context(nc.sbuf_tensor(name, shape, dt))

        def bank(name):
            return ctx.enter_context(nc.psum_tensor(name, [P, N], F32))

        def sem(name):
            return ctx.enter_context(nc.semaphore(name))

        idx_raw = sb("idx_raw", [P, TILES * TABLES], I32)
        idx_neg = sb("idx_neg", [P, TILES * TABLES], I32)
        idx_all = sb("idx_all", [P, TILES * TABLES], I32)
        idx_base = sb("idx_base", [P, TILES * TABLES], I32)
        idx_tile = sb("idx_tile", [P, TABLES], I32)
        ident = sb("ident", [P, P])
        dense_sb = sb("dense_sb", [DENSE, B])
        bw0 = sb("bw0", [DENSE, BOT0])
        bw1 = sb("bw1", [P, C0, BOT1])
        bw2 = sb("bw2", [P, C1, D])
        bb0 = sb("bb0", [P, C0])
        bb1 = sb("bb1", [P, C1])
        bb2 = sb("bb2", [P, 1])
        w0x = sb("w0x", [P, H])
        b1_row = sb("b1_row", [P, H])
        w2_row = sb("w2_row", [P, H])
        b2_col = sb("b2_col", [P, 1])
        stage = sb("stage", [P, 2, H])
        w_hi = sb("w_hi", [P, WCHUNKS, H], F32R)
        w_lo = sb("w_lo", [P, WCHUNKS, H], F32R)
        rows = sb("rows", [P, TABLES, D])
        t_hi = sb("t_hi", [P, G, S, SLOTS], F32R)
        t_lo = sb("t_lo", [P, G, S, SLOTS], F32R)
        x_t = sb("x_t", [P, B])
        xpart = sb("xpart", [P, TILES, H])
        zs = sb("zs", [P, NF, G])
        feat = sb("feat", [FC * G, S, KZ])
        r_hi = sb("r_hi", [KZ, FC, S, G], F32R)
        r_lo = sb("r_lo", [KZ, FC, S, G], F32R)
        h0 = sb("h0", [P, H])
        h0_hi = sb("h0_hi", [P, HC, P], F32R)
        h0_lo = sb("h0_lo", [P, HC, P], F32R)
        h1 = sb("h1", [P, N])
        dots = sb("dots", [P, NH])
        logits = sb("logits", [P, TILES])
        probs = sb("probs", [TILES, P])
        bx0 = xpart[:, 0:2, :].rearrange("p a (b n) -> p (a b) n", n=B)
        bx1 = xpart[:, 2:3, :].rearrange("p a (b n) -> p (a b) n", n=B)
        b0_row = h0

        em = [bank(f"em{i}") for i in range(2)]
        zz = [bank(f"zz{i}") for i in range(2)]
        xx = [bank(f"xx{i}") for i in range(2)]
        mm = [bank(f"mm{i}") for i in range(2)]

        idx_in = sem("idx_in")
        bot0_in = sem("bot0_in")
        bot1_in = sem("bot1_in")
        w0x_in = sem("w0x_in")
        last_in = sem("last_in")
        stage_in = [sem(f"stage_in{i}") for i in range(2)]
        row_in = [sem(f"row_in{t}") for t in range(TABLES)]
        out_done = sem("out_done")
        const_step = sem("const_step")
        consts = sem("consts")
        idx_copied = sem("idx_copied")
        bot_mm = sem("bot_mm")
        xp_mm = sem("xp_mm")
        em_mm = sem("em_mm")
        z_mm = sem("z_mm")
        ra_mm = sem("ra_mm")
        rb_mm = sem("rb_mm")
        l0_mm = sem("l0_mm")
        h0_mm = sem("h0_mm")
        l1_mm = sem("l1_mm")
        lt_mm = sem("lt_mm")
        bot_act = sem("bot_act")
        w_hi_done = sem("w_hi_done")
        x_hi_done = sem("x_hi_done")
        em_hi_done = sem("em_hi_done")
        z_act = sem("z_act")
        ra_act = sem("ra_act")
        r_hi_done = sem("r_hi_done")
        h0_hi_done = sem("h0_hi_done")
        probs_done = sem("probs_done")
        idx_step = sem("idx_step")
        zeroed = sem("zeroed")
        bot_dve = sem("bot_dve")
        w_lo_done = sem("w_lo_done")
        x_lo_done = sem("x_lo_done")
        em_lo_done = sem("em_lo_done")
        z_dve = sem("z_dve")
        ra_dve = sem("ra_dve")
        r_lo_done = sem("r_lo_done")
        h0_done = sem("h0_done")
        h0_lo_done = sem("h0_lo_done")
        mm_read = sem("mm_read")
        dot_done = sem("dot_done")
        logit_done = sem("logit_done")

        def em_src(j):
            n = len(GROUPS[j])
            return em[j % 2][:, 0:n * P].rearrange("p (t s g) -> p t s g", s=S, g=G)

        def em_dst(t, j):
            a, n = 1 + GROUPS[j][0], len(GROUPS[j])
            return t[:, :, :, a:a + n].rearrange("p g s t -> p t s g")

        def x_src(k):
            return x_t[:, bass.ds(k * P, P)].rearrange("p (s g) -> p s g", g=G)

        def x_dst(t):
            return t[:, :, :, 0].rearrange("p g s -> p s g")

        def z_src(j, s):
            q = slice(s * SLOTS, (s + 1) * SLOTS)
            return zz[j % 2][q, 0:PB * NZ].rearrange("p (g s f) -> p s g f", s=S, f=TABLES)[:, s]

        def z_dst(j, s):
            q = slice(s * SLOTS, (s + 1) * SLOTS)
            return zs[q, 1:NF, j * PB:(j + 1) * PB].rearrange("p f g -> p g f")

        def ra_bank(k):
            return (xx[0], xx[1], mm[0])[k // PB][0:FC * G, (k % PB) * P:(k % PB + 1) * P]

        def ra_src(k):
            return ra_bank(k).rearrange("p (s q) -> p s q", q=SLOTS)[:, :, 0:COUNT[k]]

        def rb_src():
            return mm[1][0:KZ, 0:S * FC * G].rearrange("p (s c g) -> p c s g", c=FC, g=G)

        block = ctx.enter_context(nc.Block())

        @block.sync
        def _(sp):
            sp.dma_start(idx_raw[:, :], idx).then_inc(idx_in, 16)
            sp.dma_start(dense_sb[:, :], dense_t).then_inc(bot0_in, 16)
            sp.dma_start(bw0[:, :], bot_w0_t).then_inc(bot0_in, 16)
            sp.dma_start(bb0[:, :], bot_b0).then_inc(bot0_in, 16)
            sp.dma_start(bw1[:, :, :], bot_w1_t.rearrange("(c p) n -> p c n", p=P)).then_inc(bot1_in, 16)
            sp.dma_start(bw2[:, :, :], bot_w2_t.rearrange("(c p) n -> p c n", p=P)).then_inc(bot1_in, 16)
            sp.dma_start(bb1[:, :], bot_b1).then_inc(bot1_in, 16)
            sp.dma_start(bb2[:, :], bot_b2).then_inc(bot1_in, 16)
            for c in range(WCHUNKS):
                if c >= 2:
                    sp.wait_ge(w_lo_done, c - 1)
                if c < FC:
                    sp.dma_start(stage[0:KZ, c % 2, :], top_w0z_t[c]).then_inc(stage_in[c % 2], 16)
                else:
                    sp.dma_start(stage[:, c % 2, :], top_w1_t[(c - FC) * P:(c - FC + 1) * P, :])\
                        .then_inc(stage_in[c % 2], 16)
                if c == 1:
                    sp.dma_start(w0x[:, :], top_w0x_t).then_inc(w0x_in, 16)
                    sp.dma_start(b0_row[:, :], top_b0.partition_broadcast(P)).then_inc(w0x_in, 16)
                    sp.dma_start(b1_row[:, :], top_b1.partition_broadcast(P)).then_inc(last_in, 16)
                    sp.dma_start(w2_row[:, :], top_w2.partition_broadcast(P)).then_inc(last_in, 16)
                    sp.dma_start(b2_col[:, :], top_b2.partition_broadcast(P)).then_inc(last_in, 16)
            sp.wait_ge(probs_done, 1)
            sp.dma_start(out.rearrange("(t p) o -> t (p o)", p=P), probs[:, :]).then_inc(out_done, 16)
            sp.wait_ge(out_done, 16)

        @block.gpsimd
        def _(gp):
            nc.gpsimd.iota(idx_base[:, :], [[0, TILES], [ROWS, TABLES]], base=0, channel_multiplier=0)\
                .then_inc(consts, 1)
            nc.gpsimd.memset(ident[:, :], 0.0).then_inc(const_step, 1)
            gp.wait_ge(const_step, 1)
            nc.gpsimd.affine_select(out=ident[:, :], in_=ident[:, :], compare_op=ALU.not_equal, fill=1.0,
                                    base=0, pattern=[[-1, P]], channel_multiplier=1).then_inc(consts, 1)

            def gather(t, index):
                nc.gpsimd.indirect_dma_start(rows[:, t, :], None, emb, bass.IndirectOffsetOnAxis(index, 0)).then_inc(row_in[t], 16)

            gp.wait_ge(idx_step, 4)
            for t in range(TABLES):
                gather(t, idx_all[:, t:t + 1])
            with gp.Fori(1, TILES) as k:
                for i, (g0, g1) in enumerate(HALVES):
                    t0, t1 = GROUPS[g0][0], GROUPS[g1 - 1][-1] + 1
                    gp.wait_ge(em_mm, NG * k - NG + g1)
                    nc.gpsimd.nop(nofuse=True)
                    nc.gpsimd.tensor_copy(idx_tile[:, t0:t1], idx_all[:, bass.ds(k * TABLES + t0, t1 - t0)])\
                        .then_inc(idx_copied, 1)
                    gp.wait_ge(idx_copied, 2 * k + i - 1)
                    nc.gpsimd.nop(nofuse=True)
                    for t in range(t0, t1):
                        gather(t, idx_tile[:, t:t + 1])

        @block.scalar
        def _(act):
            def split_weights(c):
                act.wait_ge(stage_in[c % 2], 16 * (c // 2 + 1))
                kp = KZ if c < FC else P
                nc.scalar.activation(w_hi[0:kp, c, :], stage[0:kp, c % 2, :], ACT.Copy).then_inc(w_hi_done, 1)

            def embeddings(k, j):
                act.wait_ge(em_mm, NG * k + j + 1)
                if j == 0:
                    nc.scalar.activation(x_dst(t_hi), x_src(k), ACT.Copy).then_inc(x_hi_done, 1)
                nc.scalar.activation(em_dst(t_hi, j), em_src(j), ACT.Copy).then_inc(em_hi_done, 1)

            def relu_bias(dst, src, bias):
                nc.scalar.activation(dst, src, ACT.Relu, bias=bias).then_inc(bot_act, 1)

            act.wait_ge(bot0_in, 48)
            act.wait_ge(bot_mm, 1)
            relu_bias(bx0[:, 0, :], mm[0][:, :], bb0[:, 0:1])
            act.wait_ge(bot_mm, 3)
            relu_bias(bx0[:, 2, :], xx[0][:, :], bb0[:, 2:3])
            split_weights(0)
            act.wait_ge(bot1_in, 64)
            act.wait_ge(bot_mm, C0 + 1)
            relu_bias(bx1[:, 0, :], zz[0][:, :], bb1[:, 0:1])
            act.wait_ge(bot_mm, C0 + C1 + 1)
            relu_bias(x_t[:, :], em[0][:, :], bb2[:, 0:1])
            act.wait_ge(zeroed, 2)
            act.wait_ge(bot_act, 4)
            for j in range(NG):
                split_weights(j + 1)
                embeddings(0, j)
            for c in range(NG + 1, WCHUNKS):
                split_weights(c)

            def tile(k, more):
                for j in range(0, ZBANKS, 2):
                    act.wait_ge(z_mm, ZBANKS * k + j + 1)
                    for s in range(S):
                        last = nc.scalar.activation(z_dst(j, s), z_src(j, s), ACT.Copy)
                    last.then_inc(z_act, 1)
                act.wait_ge(ra_mm, 3 * k + 1)
                for i in range(PB):
                    last = nc.scalar.activation(feat[:, :, OFF[i]:OFF[i + 1]], ra_src(i), ACT.Copy)
                last.then_inc(ra_act, 1)
                act.wait_ge(ra_mm, 3 * k + 3)
                nc.scalar.activation(feat[:, :, OFF[FK - 1]:KZ], ra_src(FK - 1), ACT.Copy).then_inc(ra_act, 1)
                if more:
                    embeddings(k + 1, 0)
                act.wait_ge(rb_mm, k + 1)
                nc.scalar.activation(r_hi[:, :, :, :], rb_src(), ACT.Copy).then_inc(r_hi_done, 1)
                if more:
                    embeddings(k + 1, 1)
                for h in range(2):
                    act.wait_ge(h0_mm, 2 * k + h + 1)
                    nc.scalar.activation(h0_hi[:, PB * h:PB * (h + 1), :], xx[h][:, :], ACT.Relu)\
                        .then_inc(h0_hi_done, 1)
                    if more:
                        embeddings(k + 1, 2 + h)
                if more:
                    for j in range(4, NG):
                        embeddings(k + 1, j)

            with act.Fori(0, TILES - 1) as k:
                tile(k, True)
            tile(TILES - 1, False)

            act.wait_ge(lt_mm, 1)
            act.wait_ge(last_in, 48)
            nc.scalar.activation(probs[:, :], zz[0][0:TILES, 0:P], ACT.Sigmoid, bias=b2_col[0:TILES, 0:1])\
                .then_inc(probs_done, 1)

        @block.vector
        def _(dve):
            dve.wait_ge(idx_in, 16)
            nc.vector.tensor_scalar(idx_neg[:, :], idx_raw[:, :], 0, ROWS, ALU.is_lt, ALU.mult).then_inc(idx_step, 1)
            dve.wait_ge(idx_step, 1)
            nc.vector.tensor_tensor(idx_all[:, :], idx_raw[:, :], idx_neg[:, :], ALU.add).then_inc(idx_step, 1)
            dve.wait_ge(idx_step, 2)
            nc.vector.tensor_scalar(idx_neg[:, :], idx_all[:, :], 0, ROWS - 1, ALU.max, ALU.min).then_inc(idx_step, 1)
            dve.wait_ge(consts, 1)
            dve.wait_ge(idx_step, 3)
            nc.vector.tensor_tensor(idx_all[:, :], idx_neg[:, :], idx_base[:, :], ALU.add).then_inc(idx_step, 1)
            nc.vector.memset(t_hi[:, :, :, NF:SLOTS].bitcast(F32), 0.0).then_inc(zeroed, 1)
            nc.vector.memset(t_lo[:, :, :, NF:SLOTS].bitcast(F32), 0.0).then_inc(zeroed, 1)
            nc.vector.memset(zs[:, 0, :], 0.0).then_inc(zeroed, 1)

            def split_weights(c):
                dve.wait_ge(w_hi_done, c + 1)
                kp = KZ if c < FC else P
                nc.vector.tensor_tensor(w_lo[0:kp, c, :], stage[0:kp, c % 2, :], w_hi[0:kp, c, :].bitcast(F32),
                                        ALU.subtract).then_inc(w_lo_done, 1)

            def embeddings(k, j):
                if j == 0:
                    dve.wait_ge(x_hi_done, k + 1)
                    nc.vector.tensor_tensor(x_dst(t_lo), x_src(k), x_dst(t_hi).bitcast(F32), ALU.subtract)\
                        .then_inc(x_lo_done, 1)
                dve.wait_ge(em_hi_done, NG * k + j + 1)
                nc.vector.tensor_tensor(em_dst(t_lo, j), em_src(j), em_dst(t_hi, j).bitcast(F32), ALU.subtract)\
                    .then_inc(em_lo_done, 1)

            def relu_bias(dst, src, bias):
                nc.vector.tensor_scalar(dst, src, bias, 0.0, ALU.add, ALU.max).then_inc(bot_dve, 1)

            dve.wait_ge(bot0_in, 48)
            dve.wait_ge(bot_mm, 2)
            relu_bias(bx0[:, 1, :], mm[1][:, :], bb0[:, 1:2])
            dve.wait_ge(bot_mm, 4)
            relu_bias(bx0[:, 3, :], xx[1][:, :], bb0[:, 3:4])
            split_weights(0)
            dve.wait_ge(bot1_in, 64)
            dve.wait_ge(bot_mm, C0 + C1)
            relu_bias(bx1[:, 1, :], zz[1][:, :], bb1[:, 1:2])
            dve.wait_ge(w0x_in, 32)

            def first_layer_x(i):
                for n in range(NH):
                    dve.wait_ge(xp_mm, NH * i + n + 1)
                    nc.vector.tensor_tensor(xpart[:, i, n * N:(n + 1) * N], mm[n][:, :],
                                            b0_row[:, n * N:(n + 1) * N], ALU.add).then_inc(mm_read, 1)

            for j in range(NG):
                split_weights(j + 1)
                if j < TILES:
                    first_layer_x(j)
                embeddings(0, j)
            for c in range(NG + 1, WCHUNKS):
                split_weights(c)
            dve.wait_ge(mm_read, NH * TILES)
            dve.wait_ge(last_in, 48)

            def tile(k, more):
                for j in range(1, ZBANKS, 2):
                    dve.wait_ge(z_mm, ZBANKS * k + j + 1)
                    for s in range(S):
                        last = nc.vector.tensor_copy(z_dst(j, s), z_src(j, s))
                    last.then_inc(z_dve, 1)
                dve.wait_ge(ra_mm, 3 * k + 2)
                for i in range(PB, 2 * PB):
                    last = nc.vector.tensor_copy(feat[:, :, OFF[i]:OFF[i + 1]], ra_src(i))
                last.then_inc(ra_dve, 1)
                if more:
                    embeddings(k + 1, 0)
                dve.wait_ge(r_hi_done, k + 1)
                for c in range(FC):
                    last = nc.vector.tensor_tensor(r_lo[:, c], rb_src()[:, c], r_hi[:, c].bitcast(F32), ALU.subtract)
                last.then_inc(r_lo_done, 1)
                for n in range(NH):
                    dve.wait_ge(l0_mm, NH * k + n + 1)
                    nc.vector.tensor_tensor(h0[:, n * N:(n + 1) * N], mm[n][:, :],
                                            xpart[:, bass.ds(k, 1), n * N:(n + 1) * N].rearrange("p a n -> p (a n)"),
                                            ALU.add).then_inc(h0_done, 1)
                    if more and n == 0:
                        embeddings(k + 1, 1)
                for h in range(2):
                    dve.wait_ge(h0_hi_done, 2 * k + h + 1)
                    nc.vector.scalar_tensor_tensor(h0_lo[:, PB * h:PB * (h + 1), :], xx[h][:, :], 0.0,
                                                   h0_hi[:, PB * h:PB * (h + 1), :].bitcast(F32),
                                                   ALU.max, ALU.subtract).then_inc(h0_lo_done, 1)
                    if more:
                        embeddings(k + 1, 2 + h)
                for n in range(NH):
                    dve.wait_ge(l1_mm, NH * k + n + 1)
                    if n == 1:
                        dve.wait_ge(dot_done, NH * k + 1)
                    nc.vector.tensor_tensor(h1[:, :], mm[n][:, :], b1_row[:, n * N:(n + 1) * N], ALU.add)\
                        .then_inc(mm_read, 1)
                    dve.wait_ge(mm_read, NH * (TILES + k) + n + 1)
                    nc.vector.scalar_tensor_tensor(h1[:, :], h1[:, :], 0.0, w2_row[:, n * N:(n + 1) * N],
                                                   ALU.max, ALU.mult, accum_out=dots[:, n:n + 1])\
                        .then_inc(dot_done, 1)
                    if more and n == 0:
                        embeddings(k + 1, 4)
                dve.wait_ge(dot_done, NH * (k + 1))
                nc.vector.tensor_tensor(logits[:, bass.ds(k, 1)], dots[:, 0:1], dots[:, 1:2], ALU.add)\
                    .then_inc(logit_done, 1)
                if more:
                    for j in range(5, NG):
                        embeddings(k + 1, j)

            with dve.Fori(0, TILES - 1) as k:
                tile(k, True)
            tile(TILES - 1, False)

        @block.tensor
        def _(pe):
            pe.wait_ge(bot0_in, 48)
            for m, b in enumerate((mm[0], mm[1], xx[0], xx[1])):
                nc.tensor.matmul(b[:, :], bw0[:, m * P:(m + 1) * P], dense_sb[:, :], start=True, stop=True)\
                    .then_inc(bot_mm, 1)
            pe.wait_ge(bot1_in, 64)
            pe.wait_ge(bot_act, 2)
            pe.wait_ge(bot_dve, 2)
            for m in range(C1):
                for c in range(C0):
                    last = nc.tensor.matmul(zz[m][:, :], bw1[:, c, m * P:(m + 1) * P], bx0[:, c, :],
                                            start=(c == 0), stop=(c == C0 - 1))
                last.then_inc(bot_mm, 1)
            pe.wait_ge(bot_act, 3)
            pe.wait_ge(bot_dve, 3)
            for c in range(C1):
                last = nc.tensor.matmul(em[0][:, :], bw2[:, c, :], bx1[:, c, :], start=(c == 0), stop=(c == C1 - 1))
            last.then_inc(bot_mm, 1)

            def embeddings(k, j, prior=True):
                for t in GROUPS[j]:
                    pe.wait_ge(row_in[t], 16 * k + 16)
                if j >= 2:
                    pe.wait_ge(em_lo_done, NG * k + j - 1)
                elif prior:
                    pe.wait_ge(em_lo_done, NG * k)
                for i, t in enumerate(GROUPS[j]):
                    last = nc.tensor.transpose(em[j % 2][:, i * P:(i + 1) * P], rows[:, t, :], ident[:, :])
                last.then_inc(em_mm, 1)

            def first_layer_x(i):
                for n in range(NH):
                    if i > 0:
                        pe.wait_ge(mm_read, NH * i + n - 1)
                    nc.tensor.matmul(mm[n][:, :], x_t[:, i * P:(i + 1) * P], w0x[:, n * N:(n + 1) * N],
                                     start=True, stop=True).then_inc(xp_mm, 1)

            pe.wait_ge(bot_act, 4)
            pe.wait_ge(w0x_in, 32)
            pe.wait_ge(consts, 2)
            for j in range(NG):
                if j < TILES:
                    first_layer_x(j)
                embeddings(0, j, prior=False)
            pe.wait_ge(zeroed, 3)
            pe.wait_ge(mm_read, NH * TILES)

            def tile(k, more):
                pe.wait_ge(em_lo_done, NG * (k + 1))
                pe.wait_ge(x_lo_done, k + 1)
                for j in range(ZBANKS):
                    if j >= 2 and j % 2 == 0:
                        pe.wait_ge(z_act, (ZBANKS // 2) * k + j // 2)
                    elif j >= 2:
                        pe.wait_ge(z_dve, (ZBANKS // 2) * k + j // 2)
                    for g in range(PB * j, PB * (j + 1)):
                        o = zz[j % 2][:, (g % PB) * NZ:(g % PB + 1) * NZ]
                        for a, (left, right) in enumerate(((t_hi, t_hi), (t_hi, t_lo), (t_lo, t_hi))):
                            last = nc.tensor.matmul(o, left[:, g, :, :], right[:, g, :, 1:NF],
                                                    start=(a == 0), stop=(a == 2))
                    last.then_inc(z_mm, 1)
                pe.wait_ge(z_act, (ZBANKS // 2) * (k + 1))
                pe.wait_ge(z_dve, (ZBANKS // 2) * (k + 1))
                pe.wait_ge(mm_read, NH * (TILES + k))
                for i in range(FK):
                    last = nc.tensor.transpose(ra_bank(i), zs[:, FC * i:FC * (i + 1), :], ident[:, :])
                    if i % PB == PB - 1 or i == FK - 1:
                        last.then_inc(ra_mm, 1)
                if more:
                    embeddings(k + 1, 0)
                pe.wait_ge(ra_act, 2 * (k + 1))
                pe.wait_ge(ra_dve, k + 1)
                for s in range(S):
                    last = nc.tensor.transpose(mm[1][0:KZ, s * FC * G:(s + 1) * FC * G], feat[:, s, :],
                                               ident[0:FC * G, 0:FC * G])
                last.then_inc(rb_mm, 1)
                pe.wait_ge(w_lo_done, FC)
                for n in range(NH):
                    cols = slice(n * N, (n + 1) * N)
                    if n == 0:
                        pe.wait_ge(r_hi_done, k + 1)
                    for a, (r, w) in enumerate(((r_hi, w_hi), (r_hi, w_lo), (r_lo, w_hi))):
                        if n == 0 and a == 2:
                            pe.wait_ge(r_lo_done, k + 1)
                        for c in range(FC):
                            last = nc.tensor.matmul(mm[n][:, :], r[:, c, :, :], w[0:KZ, c, cols],
                                                    start=(a == 0 and c == 0), stop=(a == 2 and c == FC - 1))
                    last.then_inc(l0_mm, 1)
                    if more and n == 0:
                        embeddings(k + 1, 1)
                for h in range(2):
                    pe.wait_ge(h0_done, 2 * k + h + 1)
                    for c in range(PB):
                        q = PB * h + c
                        last = nc.tensor.transpose(xx[h][:, c * P:(c + 1) * P], h0[:, q * P:(q + 1) * P], ident[:, :])
                    last.then_inc(h0_mm, 1)
                    if more:
                        embeddings(k + 1, 2 + h)
                pe.wait_ge(w_lo_done, WCHUNKS)
                for n in range(NH):
                    cols = slice(n * N, (n + 1) * N)
                    steps = [(h0_hi, w, c) for h in range(2) for w in (w_hi, w_lo)
                             for c in range(PB * h, PB * (h + 1))]
                    steps += [(h0_lo, w_hi, c) for c in range(HC)]
                    for a, (r, w, c) in enumerate(steps):
                        if n == 0 and a in (0, 2 * PB):
                            pe.wait_ge(h0_hi_done, 2 * k + a // (2 * PB) + 1)
                        if n == 0 and a == 2 * HC:
                            pe.wait_ge(h0_lo_done, 2 * k + 2)
                        last = nc.tensor.matmul(mm[n][:, :], r[:, c, :], w[:, FC + c, cols],
                                                start=(a == 0), stop=(a == len(steps) - 1))
                    last.then_inc(l1_mm, 1)
                    if more and n == 0:
                        embeddings(k + 1, 4)
                if more:
                    for j in range(5, NG):
                        embeddings(k + 1, j)

            with pe.Fori(0, TILES - 1) as k:
                tile(k, True)
            tile(TILES - 1, False)

            pe.wait_ge(logit_done, TILES)
            nc.tensor.transpose(zz[0][0:TILES, 0:P], logits[:, :], ident[:, :]).then_inc(lt_mm, 1)


def kernel(**inputs):
    import numpy as np
    import concourse.bacc as bacc
    from concourse.bass_utils import run_bass_kernel_spmd

    def get(name):
        return np.asarray(inputs[name])

    def cols(b):
        return np.ascontiguousarray(b.reshape(-1, P).T)

    w0 = get("L0_rec_top_w0")
    w0z = np.zeros((FC, KZ, H), w0.dtype)
    for f in range(1, NF):
        at = D + f * (f - 1) // 2
        c, k = f % FC, f // FC
        w0z[c, OFF[k]:OFF[k] + f, :] = w0[:, at:at + f].T
    idx = get("r_lS_i").reshape(TABLES, TILES, P).transpose(2, 1, 0).reshape(P, TILES * TABLES)
    arrays = {
        "idx": np.ascontiguousarray(idx),
        "dense_t": np.ascontiguousarray(get("r_dense_x").T),
        "bot_w0_t": np.ascontiguousarray(get("L0_rec_bot_w0").T),
        "bot_b0": cols(get("L0_rec_bot_b0")),
        "bot_w1_t": np.ascontiguousarray(get("L0_rec_bot_w1").T),
        "bot_b1": cols(get("L0_rec_bot_b1")),
        "bot_w2_t": np.ascontiguousarray(get("L0_rec_bot_w2").T),
        "bot_b2": cols(get("L0_rec_bot_b2")),
        "top_w0x_t": np.ascontiguousarray(w0[:, 0:D].T),
        "top_w0z_t": w0z,
        "top_b0": get("L0_rec_top_b0"),
        "top_w1_t": np.ascontiguousarray(get("L0_rec_top_w1").T),
        "top_b1": get("L0_rec_top_b1"),
        "top_w2": get("L0_rec_top_w2").reshape(-1),
        "top_b2": get("L0_rec_top_b2"),
        "emb": get("L0_rec_emb_W").reshape(TABLES * ROWS, D),
    }
    nc = bacc.Bacc("TRN2", target_bir_lowering=False, num_devices=1)
    args = {n: nc.dram_tensor(f"in_{n}", a.shape, mybir.dt.from_np(a.dtype), kind="ExternalInput").ap()
            for n, a in arrays.items()}
    out = nc.dram_tensor("out", (B, 1), F32, kind="ExternalOutput").ap()
    program(nc, out=out, **args)
    r = run_bass_kernel_spmd(nc, [{f"in_{n}": a for n, a in arrays.items()}], core_ids=[0])
    return r.results[0]["out"]
```

```python
from contextlib import ExitStack

import concourse.bass as bass
from concourse import mybir

F32 = mybir.dt.float32
F32R = mybir.dt.float32r
I32 = mybir.dt.int32
ACT = mybir.ActivationFunctionType
ALU = mybir.AluOpType

P = 128
B = 512
TILES = B // P
D = 128
TABLES = 26
ROWS = 12500
SLOTS = 32
NF = 1 + TABLES
S = P // SLOTS
G = P // S
PB = 4
ZBANKS = G // PB
NZ = S * TABLES
FC = 3
FK = NF // FC
COUNT = [FC * k + FC - 1 for k in range(FK)]
OFF = [sum(COUNT[:k]) for k in range(FK + 1)]
KZ = OFF[FK]
H = 1024
HC = H // P
N = 512
NH = H // N
DENSE, BOT0, BOT1 = 13, 512, 256
C0, C1 = BOT0 // P, BOT1 // P
GROUPS = [list(range(t, min(t + PB, TABLES))) for t in range(0, TABLES, PB)]
NG = len(GROUPS)
HALVES = [(0, 4), (4, NG)]
EA, ED = (NG + 1) // 2, NG // 2
L1_STEPS = [(a, w, c) for h in range(2) for a, w in (("hi", "hi"), ("hi", "lo")) for c in range(PB * h, PB * (h + 1))]
L1_STEPS += [("lo", "hi", c) for c in range(HC)]
L1_HELD = {"z": 14, "ra": 17, "rb": 20}
AMONG = {(0, 8): 2, (0, 16): 3, (1, 0): 4, (1, 4): 5, (1, 9): 6}
STAGES = 8
PIECES = [(c, n) for n in range(NH) for c in range(FC)] + [(FC + c, n) for n in range(NH) for c in range(HC)]


def program(nc, idx, bot_first, bot_biases, bot_rest, top_w0x_t, top_w0z_t, top_b0, top_w1_t, top_b1, top_w2, top_b2, emb, out):
    with ExitStack() as ctx:
        def sb(name, shape, dt=F32):
            return ctx.enter_context(nc.sbuf_tensor(name, shape, dt))

        def bank(name):
            return ctx.enter_context(nc.psum_tensor(name, [P, N], F32))

        def sem(name):
            return ctx.enter_context(nc.semaphore(name))

        idx_raw = sb("idx_raw", [P, TILES * TABLES], I32)
        idx_neg = sb("idx_neg", [P, TILES * TABLES], I32)
        idx_all = sb("idx_all", [P, TILES * TABLES], I32)
        idx_base = sb("idx_base", [P, TILES * TABLES], I32)
        idx_tile = sb("idx_tile", [P, TABLES], I32)
        ident = sb("ident", [P, P])
        bot_a = sb("bot_a", [DENSE, B + BOT0])
        dense_sb, bw0 = bot_a[:, 0:B], bot_a[:, B:B + BOT0]
        bot_b = sb("bot_b", [P, C0 + C1 + 1])
        bb0, bb1, bb2 = bot_b[:, 0:C0], bot_b[:, C0:C0 + C1], bot_b[:, C0 + C1:C0 + C1 + 1]
        bot_c = sb("bot_c", [P, C0 * BOT1 + C1 * D])
        bw1 = bot_c[:, 0:C0 * BOT1].rearrange("p (c n) -> p c n", n=BOT1)
        bw2 = bot_c[:, C0 * BOT1:].rearrange("p (c n) -> p c n", n=D)
        w0x = sb("w0x", [P, H])
        b1_row = sb("b1_row", [1, H])
        b1_parts = sb("b1_parts", [P, H], F32R)
        ones_f = sb("ones_f", [P, P])
        ones = sb("ones", [P, P], F32R)
        w2_row = sb("w2_row", [P, H])
        b2_col = sb("b2_col", [P, 1])
        stage = sb("stage", [P, STAGES, N])
        w_hi = sb("w_hi", [P, FC + HC, H], F32R)
        w_lo = sb("w_lo", [P, FC + HC, H], F32R)
        rows = sb("rows", [P, TABLES, D])
        vecs = sb("vecs", [P, G, S, SLOTS])
        x_t = sb("x_t", [P, B])
        xpart = sb("xpart", [P, TILES, H])
        zs = sb("zs", [P, NF, G])
        feat = sb("feat", [FC * G, S, KZ])
        r_hi = sb("r_hi", [KZ, FC, S, G], F32R)
        r_lo = sb("r_lo", [KZ, FC, S, G], F32R)
        h0 = sb("h0", [P, H])
        h0_hi = sb("h0_hi", [P, HC, P], F32R)
        h0_lo = sb("h0_lo", [P, HC, P], F32R)
        dots = sb("dots", [P, NH, TILES])
        probs = sb("probs", [TILES, P])
        bx0 = xpart[:, 0:2, :].rearrange("p a (b n) -> p (a b) n", n=B)
        bx1 = xpart[:, 2:3, :].rearrange("p a (b n) -> p (a b) n", n=B)
        b0_row = h0
        h1 = h0

        em = [bank(f"em{i}") for i in range(2)]
        zz = [bank(f"zz{i}") for i in range(2)]
        xx = [bank(f"xx{i}") for i in range(2)]
        mm = [bank(f"mm{i}") for i in range(2)]

        idx_in = sem("idx_in")
        bot0_in = sem("bot0_in")
        bot1_in = sem("bot1_in")
        bot2_in = sem("bot2_in")
        w0x_in = sem("w0x_in")
        last_in = sem("last_in")
        stage_in = [sem(f"stage_in{i}") for i in range(STAGES)]
        row_in = [sem(f"row_in{t}") for t in range(TABLES)]
        out_done = sem("out_done")
        const_step = sem("const_step")
        consts = sem("consts")
        idx_copied = sem("idx_copied")
        bot_mm = sem("bot_mm")
        xp_mm = sem("xp_mm")
        em_mm = sem("em_mm")
        z_mm = sem("z_mm")
        ra_mm = sem("ra_mm")
        rb_mm = sem("rb_mm")
        l0_mm = sem("l0_mm")
        h0_mm = sem("h0_mm")
        l1_mm = sem("l1_mm")
        lt_mm = sem("lt_mm")
        bot_act = sem("bot_act")
        w_hi_done = sem("w_hi_done")
        b1_hi_done = sem("b1_hi_done")
        em_act = sem("em_act")
        z_act = sem("z_act")
        ra_act = sem("ra_act")
        r_hi_done = sem("r_hi_done")
        h0_hi_done = sem("h0_hi_done")
        probs_done = sem("probs_done")
        idx_step = sem("idx_step")
        ones_set = sem("ones_set")
        zeroed = sem("zeroed")
        bot_dve = sem("bot_dve")
        w_lo_done = sem("w_lo_done")
        b1_lo_done = sem("b1_lo_done")
        em_dve = sem("em_dve")
        z_dve = sem("z_dve")
        ra_dve = sem("ra_dve")
        r_lo_done = sem("r_lo_done")
        h0_done = sem("h0_done")
        h0_lo_done = sem("h0_lo_done")
        mm_read = sem("mm_read")

        def em_src(j):
            n = len(GROUPS[j])
            return em[j % 2][:, 0:n * P].rearrange("p (t s g) -> p t s g", s=S, g=G)

        def em_dst(j):
            a, n = 1 + GROUPS[j][0], len(GROUPS[j])
            return vecs[:, :, :, a:a + n].rearrange("p g s t -> p t s g")

        def x_src(k):
            return x_t[:, bass.ds(k * P, P)].rearrange("p (s g) -> p s g", g=G)

        def x_dst():
            return vecs[:, :, :, 0].rearrange("p g s -> p s g")

        z_banks = (*zz, *xx)
        ra_banks = (*zz, xx[0])
        rb_bank = xx[1]

        def xp_bank(i, n):
            return (mm, xx)[i % 2][n]

        def z_src(j, s):
            q = slice(s * SLOTS, (s + 1) * SLOTS)
            return z_banks[j % 4][q, 0:PB * NZ].rearrange("p (g s f) -> p s g f", s=S, f=TABLES)[:, s]

        def z_dst(j, s):
            q = slice(s * SLOTS, (s + 1) * SLOTS)
            return zs[q, 1:NF, j * PB:(j + 1) * PB].rearrange("p f g -> p g f")

        def ra_bank(k):
            return ra_banks[k // PB][0:FC * G, (k % PB) * P:(k % PB + 1) * P]

        def ra_src(k):
            return ra_bank(k).rearrange("p (s q) -> p s q", q=SLOTS)[:, :, 0:COUNT[k]]

        def rb_src():
            return rb_bank[0:KZ, 0:S * FC * G].rearrange("p (s c g) -> p c s g", c=FC, g=G)

        block = ctx.enter_context(nc.Block())

        @block.sync
        def _(sp):
            sp.dma_start(idx_raw[:, :], idx).then_inc(idx_in, 16)
            sp.dma_start(bot_a[:, :], bot_first).then_inc(bot0_in, 16)
            sp.dma_start(bot_c[:, :], bot_rest).then_inc(bot2_in, 16)
            sp.dma_start(bot_b[:, :], bot_biases).then_inc(bot1_in, 16)
            sp.dma_start(w0x[:, :], top_w0x_t).then_inc(w0x_in, 16)
            sp.dma_start(b0_row[:, :], top_b0.partition_broadcast(P)).then_inc(w0x_in, 16)
            for i, (c, n) in enumerate(PIECES):
                if i >= STAGES:
                    sp.wait_ge(w_lo_done, i - STAGES + 1)
                cols = slice(n * N, (n + 1) * N)
                if c < FC:
                    sp.dma_start(stage[0:KZ, i % STAGES, :], top_w0z_t[c, :, cols]).then_inc(stage_in[i % STAGES], 16)
                else:
                    sp.dma_start(stage[:, i % STAGES, :], top_w1_t[(c - FC) * P:(c - FC + 1) * P, cols])\
                        .then_inc(stage_in[i % STAGES], 16)
                if i == STAGES - 1:
                    sp.dma_start(b1_row[:, :], top_b1.rearrange("(o n) -> o n", o=1)).then_inc(last_in, 16)
                    sp.dma_start(w2_row[:, :], top_w2.partition_broadcast(P)).then_inc(last_in, 16)
                    sp.dma_start(b2_col[:, :], top_b2.partition_broadcast(P)).then_inc(last_in, 16)
            sp.wait_ge(probs_done, 1)
            sp.dma_start(out.rearrange("(t p) o -> t (p o)", p=P), probs[:, :]).then_inc(out_done, 16)
            sp.wait_ge(out_done, 16)

        @block.gpsimd
        def _(gp):
            nc.gpsimd.iota(idx_base[:, :], [[0, TILES], [ROWS, TABLES]], base=0, channel_multiplier=0)\
                .then_inc(consts, 1)
            nc.gpsimd.memset(ident[:, :], 0.0).then_inc(const_step, 1)
            gp.wait_ge(const_step, 1)
            nc.gpsimd.affine_select(out=ident[:, :], in_=ident[:, :], compare_op=ALU.not_equal, fill=1.0,
                                    base=0, pattern=[[-1, P]], channel_multiplier=1).then_inc(consts, 1)

            def gather(t, index):
                nc.gpsimd.indirect_dma_start(rows[:, t, :], None, emb, bass.IndirectOffsetOnAxis(index, 0)).then_inc(row_in[t], 16)

            gp.wait_ge(idx_step, 3)
            for t in range(TABLES):
                gather(t, idx_all[:, t:t + 1])
            with gp.Fori(1, TILES) as k:
                for i, (g0, g1) in enumerate(HALVES):
                    t0, t1 = GROUPS[g0][0], GROUPS[g1 - 1][-1] + 1
                    gp.wait_ge(em_mm, NG * k - NG + g1)
                    nc.gpsimd.nop(nofuse=True)
                    nc.gpsimd.tensor_copy(idx_tile[:, t0:t1], idx_all[:, bass.ds(k * TABLES + t0, t1 - t0)])\
                        .then_inc(idx_copied, 1)
                    gp.wait_ge(idx_copied, 2 * k + i - 1)
                    nc.gpsimd.nop(nofuse=True)
                    for t in range(t0, t1):
                        gather(t, idx_tile[:, t:t + 1])

        @block.scalar
        def _(act):
            def split_weights(first, end):
                for i in range(first, end):
                    c, n = PIECES[i]
                    kp = KZ if c < FC else P
                    act.wait_ge(stage_in[i % STAGES], 16 * (i // STAGES + 1))
                    nc.scalar.activation(w_hi[0:kp, c, n * N:(n + 1) * N], stage[0:kp, i % STAGES, :], ACT.Copy)\
                        .then_inc(w_hi_done, 1)

            def embeddings(k, j):
                act.wait_ge(em_mm, NG * k + j + 1)
                if j == 0:
                    nc.scalar.activation(x_dst(), x_src(k), ACT.Copy)
                nc.scalar.activation(em_dst(j), em_src(j), ACT.Copy).then_inc(em_act, 1)

            def relu_bias(dst, src, bias):
                nc.scalar.activation(dst, src, ACT.Relu, bias=bias).then_inc(bot_act, 1)

            act.wait_ge(ones_set, 1)
            nc.scalar.activation(ones[:, :], ones_f[:, :], ACT.Copy).then_inc(b1_hi_done, 1)
            act.wait_ge(bot1_in, 16)
            act.wait_ge(bot_mm, 1)
            relu_bias(bx0[:, 0, :], mm[0][:, :], bb0[:, 0:1])
            split_weights(0, 2)
            act.wait_ge(bot_mm, 3)
            relu_bias(bx0[:, 2, :], xx[0][:, :], bb0[:, 2:3])
            split_weights(2, 8)
            act.wait_ge(bot_mm, C0 + 1)
            relu_bias(bx1[:, 0, :], zz[0][:, :], bb1[:, 0:1])
            split_weights(8, 12)
            act.wait_ge(bot_mm, C0 + C1 + 1)
            relu_bias(x_t[:, :], mm[0][:, :], bb2[:, 0:1])
            act.wait_ge(bot_act, 4)
            embeddings(0, 0)
            act.wait_ge(last_in, 48)
            act.wait_ge(zeroed, 3)
            nc.scalar.activation(b1_parts[0:1, :], b1_row[:, :], ACT.Copy).then_inc(b1_hi_done, 1)
            embeddings(0, 2)
            split_weights(12, len(PIECES))
            embeddings(0, 4)
            embeddings(0, 6)

            def front(k):
                for j in range(0, ZBANKS, 2):
                    act.wait_ge(z_mm, ZBANKS * k + j + 1)
                    for s in range(S):
                        last = nc.scalar.activation(z_dst(j, s), z_src(j, s), ACT.Copy)
                    last.then_inc(z_act, 1)
                act.wait_ge(ra_mm, 3 * k + 2)
                for i in range(PB):
                    last = nc.scalar.activation(feat[:, :, OFF[i]:OFF[i + 1]], ra_src(i), ACT.Copy)
                last.then_inc(ra_act, 1)
                act.wait_ge(ra_mm, 3 * k + 3)
                nc.scalar.activation(feat[:, :, OFF[FK - 1]:KZ], ra_src(FK - 1), ACT.Copy).then_inc(ra_act, 1)
                act.wait_ge(rb_mm, k + 1)
                nc.scalar.activation(r_hi[:, :, :, :], rb_src(), ACT.Copy).then_inc(r_hi_done, 1)

            def back(k, more):
                if more:
                    embeddings(k + 1, 0)
                for h in range(2):
                    act.wait_ge(h0_mm, 2 * k + h + 1)
                    nc.scalar.activation(h0_hi[:, PB * h:PB * (h + 1), :], xx[h][:, :], ACT.Relu)\
                        .then_inc(h0_hi_done, 1)
                if more:
                    for j in range(2, NG, 2):
                        embeddings(k + 1, j)

            front(0)
            with act.Fori(0, TILES - 1) as k:
                back(k, True)
                front(k + 1)
            back(TILES - 1, False)

            act.wait_ge(lt_mm, 1)
            nc.scalar.activation(probs[:, :], zz[0][0:TILES, 0:P], ACT.Sigmoid, bias=b2_col[0:TILES, 0:1])\
                .then_inc(probs_done, 1)

        @block.vector
        def _(dve):
            nc.vector.memset(ones_f[:, :], 1.0).then_inc(ones_set, 1)
            nc.vector.memset(zs[:, 0, :], 0.0).then_inc(zeroed, 1)
            nc.vector.memset(vecs[:, :, :, NF:SLOTS], 0.0).then_inc(zeroed, 1)
            nc.vector.memset(b1_parts[:, :].bitcast(F32), 0.0).then_inc(zeroed, 1)
            dve.wait_ge(idx_in, 16)
            nc.vector.tensor_scalar(idx_neg[:, :], idx_raw[:, :], 0, ROWS, ALU.is_lt, ALU.mult).then_inc(idx_step, 1)
            dve.wait_ge(idx_step, 1)
            nc.vector.scalar_tensor_tensor(idx_raw[:, :], idx_raw[:, :], -ROWS, idx_neg[:, :], ALU.max, ALU.add)\
                .then_inc(idx_step, 1)
            dve.wait_ge(consts, 1)
            dve.wait_ge(idx_step, 2)
            nc.vector.scalar_tensor_tensor(idx_all[:, :], idx_raw[:, :], ROWS - 1, idx_base[:, :], ALU.min, ALU.add)\
                .then_inc(idx_step, 1)

            def split_weights(first, end):
                for i in range(first, end):
                    c, n = PIECES[i]
                    kp = KZ if c < FC else P
                    cols = slice(n * N, (n + 1) * N)
                    dve.wait_ge(w_hi_done, i + 1)
                    nc.vector.tensor_tensor(w_lo[0:kp, c, cols], stage[0:kp, i % STAGES, :],
                                            w_hi[0:kp, c, cols].bitcast(F32), ALU.subtract).then_inc(w_lo_done, 1)

            def embeddings(k, j):
                dve.wait_ge(em_mm, NG * k + j + 1)
                nc.vector.tensor_copy(em_dst(j), em_src(j)).then_inc(em_dve, 1)

            def relu_bias(dst, src, bias):
                nc.vector.tensor_scalar(dst, src, bias, 0.0, ALU.add, ALU.max).then_inc(bot_dve, 1)

            dve.wait_ge(bot1_in, 16)
            dve.wait_ge(bot_mm, 2)
            relu_bias(bx0[:, 1, :], mm[1][:, :], bb0[:, 1:2])
            split_weights(0, 2)
            dve.wait_ge(bot_mm, 4)
            relu_bias(bx0[:, 3, :], xx[1][:, :], bb0[:, 3:4])
            split_weights(2, 8)
            dve.wait_ge(bot_mm, C0 + C1)
            relu_bias(bx1[:, 1, :], zz[1][:, :], bb1[:, 1:2])
            dve.wait_ge(w0x_in, 32)

            def first_layer_x(i):
                for n in range(NH):
                    dve.wait_ge(xp_mm, NH * i + n + 1)
                    nc.vector.tensor_tensor(xpart[:, i, n * N:(n + 1) * N], xp_bank(i, n)[:, :],
                                            b0_row[:, n * N:(n + 1) * N], ALU.add).then_inc(mm_read, 1)

            split_weights(8, 10)
            embeddings(0, 1)
            first_layer_x(0)
            split_weights(10, 12)
            first_layer_x(1)
            split_weights(12, 14)
            embeddings(0, 3)
            first_layer_x(2)
            dve.wait_ge(b1_hi_done, 2)
            nc.vector.tensor_tensor(b1_parts[32:33, :], b1_row[:, :], b1_parts[0:1, :].bitcast(F32), ALU.subtract)\
                .then_inc(b1_lo_done, 1)
            split_weights(14, 16)
            first_layer_x(3)
            embeddings(0, 5)
            dve.wait_ge(last_in, 48)

            def front(k, pieces=()):
                for j in range(1, ZBANKS, 2):
                    dve.wait_ge(z_mm, ZBANKS * k + j + 1)
                    for s in range(S):
                        last = nc.vector.tensor_copy(z_dst(j, s), z_src(j, s))
                    last.then_inc(z_dve, 1)
                    for i in pieces[j // 2:j // 2 + 1]:
                        split_weights(i, i + 1)
                dve.wait_ge(ra_mm, 3 * k + 1)
                for i in range(PB, 2 * PB):
                    last = nc.vector.tensor_copy(feat[:, :, OFF[i]:OFF[i + 1]], ra_src(i))
                last.then_inc(ra_dve, 1)
                dve.wait_ge(r_hi_done, k + 1)
                for c in range(FC):
                    last = nc.vector.tensor_tensor(r_lo[:, c], rb_src()[:, c], r_hi[:, c].bitcast(F32), ALU.subtract)
                last.then_inc(r_lo_done, 1)

            def dot(k, n):
                dve.wait_ge(l1_mm, NH * k + n + 1)
                nc.vector.scalar_tensor_tensor(h1[:, n * N:(n + 1) * N], mm[n][:, :], 0.0,
                                               w2_row[:, n * N:(n + 1) * N], ALU.max, ALU.mult,
                                               accum_out=dots[:, n, bass.ds(k, 1)]).then_inc(mm_read, 1)

            def back(k, more):
                for n in range(NH):
                    dve.wait_ge(l0_mm, NH * k + n + 1)
                    nc.vector.tensor_tensor(h0[:, n * N:(n + 1) * N], mm[n][:, :],
                                            xpart[:, bass.ds(k, 1), n * N:(n + 1) * N].rearrange("p a n -> p (a n)"),
                                            ALU.add).then_inc(h0_done, 1)
                if more:
                    embeddings(k + 1, 1)
                for h in range(2):
                    dve.wait_ge(h0_hi_done, 2 * k + h + 1)
                    nc.vector.scalar_tensor_tensor(h0_lo[:, PB * h:PB * (h + 1), :], xx[h][:, :], 0.0,
                                                   h0_hi[:, PB * h:PB * (h + 1), :].bitcast(F32),
                                                   ALU.max, ALU.subtract).then_inc(h0_lo_done, 1)
                if more:
                    embeddings(k + 1, 3)
                dot(k, 0)
                if more:
                    embeddings(k + 1, 5)

            front(0, range(16, 20))
            split_weights(20, len(PIECES))
            dve.wait_ge(mm_read, NH * TILES)
            with dve.Fori(0, TILES - 1) as k:
                back(k, True)
                front(k + 1)
                dot(k, 1)
            back(TILES - 1, False)
            dot(TILES - 1, 1)

        @block.tensor
        def _(pe):
            def embeddings(k, j, prior=True):
                for t in GROUPS[j]:
                    pe.wait_ge(row_in[t], 16 * k + 16)
                if (prior or j >= 2) and j % 2 == 0:
                    pe.wait_ge(em_act, EA * k + j // 2)
                elif prior or j >= 2:
                    pe.wait_ge(em_dve, ED * k + j // 2)
                for i, t in enumerate(GROUPS[j]):
                    last = nc.tensor.transpose(em[j % 2][:, i * P:(i + 1) * P], rows[:, t, :], ident[:, :])
                last.then_inc(em_mm, 1)

            def first_layer_x(i):
                for n in range(NH):
                    if i > 1:
                        pe.wait_ge(mm_read, NH * (i - 2) + n + 1)
                    nc.tensor.matmul(xp_bank(i, n)[:, :], x_t[:, i * P:(i + 1) * P], w0x[:, n * N:(n + 1) * N],
                                     start=True, stop=True).then_inc(xp_mm, 1)

            pe.wait_ge(bot0_in, 16)
            for m, b in enumerate((mm[0], mm[1], xx[0], xx[1])):
                nc.tensor.matmul(b[:, :], bw0[:, m * P:(m + 1) * P], dense_sb, start=True, stop=True)\
                    .then_inc(bot_mm, 1)
            pe.wait_ge(bot2_in, 16)
            for m in range(C1):
                for c in range(C0):
                    if m == 0:
                        pe.wait_ge((bot_act, bot_dve)[c % 2], c // 2 + 1)
                    last = nc.tensor.matmul(zz[m][:, :], bw1[:, c, m * P:(m + 1) * P], bx0[:, c, :],
                                            start=(c == 0), stop=(c == C0 - 1))
                last.then_inc(bot_mm, 1)
            pe.wait_ge(consts, 2)
            for c in range(C1):
                pe.wait_ge((bot_act, bot_dve)[c], 3)
                last = nc.tensor.matmul(mm[0][:, :], bw2[:, c, :], bx1[:, c, :], start=(c == 0), stop=(c == C1 - 1))
                if c == 0:
                    embeddings(0, 0, prior=False)
            last.then_inc(bot_mm, 1)
            embeddings(0, 1, prior=False)

            pe.wait_ge(bot_act, 4)
            pe.wait_ge(w0x_in, 32)
            for i in range(TILES):
                first_layer_x(i)
                if i + 2 < 5:
                    embeddings(0, i + 2)
            embeddings(0, 5)
            embeddings(0, 6)
            pe.wait_ge(zeroed, 3)
            pe.wait_ge(mm_read, NH * TILES)

            def layer1(k, n, first, end):
                cols = slice(n * N, (n + 1) * N)
                for i in range(first, end):
                    part, w_part, c = L1_STEPS[i]
                    if i == 0:
                        nc.tensor.matmul(mm[n][:, :], ones[:, :], b1_parts[:, cols], start=True, stop=False)
                    if n == 0 and i in (0, 2 * PB):
                        pe.wait_ge(h0_hi_done, 2 * k + i // (2 * PB) + 1)
                    if n == 0 and i == 2 * HC:
                        pe.wait_ge(h0_lo_done, 2 * k + 2)
                    last = nc.tensor.matmul(mm[n][:, :], (h0_hi if part == "hi" else h0_lo)[:, c, :],
                                            (w_hi if w_part == "hi" else w_lo)[:, FC + c, cols],
                                            start=False, stop=(i == len(L1_STEPS) - 1))
                if end == len(L1_STEPS):
                    last.then_inc(l1_mm, 1)

            def front(k, held):
                pe.wait_ge(em_act, EA * (k + 1))
                pe.wait_ge(em_dve, ED * (k + 1))
                for j in range(ZBANKS):
                    if j >= 4:
                        pe.wait_ge((z_act, z_dve)[j % 2], (ZBANKS // 2) * k + j // 2 - 1)
                    for g in range(PB * j, PB * (j + 1)):
                        o = z_banks[j % 4][:, (g % PB) * NZ:(g % PB + 1) * NZ]
                        last = nc.tensor.matmul(o, vecs[:, g, :, :], vecs[:, g, :, 1:NF], start=True, stop=True)
                    last.then_inc(z_mm, 1)
                if held:
                    layer1(k - 1, 1, L1_HELD["z"], L1_HELD["ra"])
                pe.wait_ge(z_act, (ZBANKS // 2) * (k + 1))
                pe.wait_ge(z_dve, (ZBANKS // 2) * (k + 1))
                for some in (range(PB, 2 * PB), range(PB), range(2 * PB, FK)):
                    for i in some:
                        last = nc.tensor.transpose(ra_bank(i), zs[:, FC * i:FC * (i + 1), :], ident[:, :])
                    last.then_inc(ra_mm, 1)
                if held:
                    layer1(k - 1, 1, L1_HELD["ra"], L1_HELD["rb"])
                pe.wait_ge(ra_act, 2 * (k + 1))
                pe.wait_ge(ra_dve, k + 1)
                for s in range(S):
                    last = nc.tensor.transpose(rb_bank[0:KZ, s * FC * G:(s + 1) * FC * G], feat[:, s, :],
                                               ident[0:FC * G, 0:FC * G])
                last.then_inc(rb_mm, 1)
                if held:
                    layer1(k - 1, 1, L1_HELD["rb"], len(L1_STEPS))

            def back(k, more):
                for n in range(NH):
                    cols = slice(n * N, (n + 1) * N)
                    pe.wait_ge(w_lo_done, FC * (n + 1))
                    pe.wait_ge(mm_read, NH * (TILES + k) + n - 1)
                    if n == 0:
                        pe.wait_ge(r_hi_done, k + 1)
                    for a, (r, w) in enumerate(((r_hi, w_hi), (r_hi, w_lo), (r_lo, w_hi))):
                        if n == 0 and a == 2:
                            pe.wait_ge(r_lo_done, k + 1)
                        for c in range(FC):
                            last = nc.tensor.matmul(mm[n][:, :], r[:, c, :, :], w[0:KZ, c, cols],
                                                    start=(a == 0 and c == 0), stop=(a == 2 and c == FC - 1))
                    last.then_inc(l0_mm, 1)
                for h in range(2):
                    pe.wait_ge(h0_done, 2 * k + h + 1)
                    for c in range(PB):
                        q = PB * h + c
                        last = nc.tensor.transpose(xx[h][:, c * P:(c + 1) * P], h0[:, q * P:(q + 1) * P], ident[:, :])
                    last.then_inc(h0_mm, 1)
                    if more and h == 0:
                        embeddings(k + 1, 0)
                        embeddings(k + 1, 1)
                for n in range(NH):
                    pe.wait_ge(w_lo_done, NH * FC + HC * (n + 1))
                    pe.wait_ge(b1_lo_done, 1)
                    end = L1_HELD["z"] if more and n == 1 else len(L1_STEPS)
                    at = 0
                    for i in sorted(i for m, i in AMONG if m == n) if more else ():
                        layer1(k, n, at, i)
                        embeddings(k + 1, AMONG[n, i])
                        at = i
                    layer1(k, n, at, end)

            front(0, False)
            with pe.Fori(0, TILES - 1) as k:
                back(k, True)
                front(k + 1, True)
            back(TILES - 1, False)
            for n in range(NH):
                pe.wait_ge(mm_read, NH * (2 * TILES - 1) + n + 1)
                last = nc.tensor.matmul(zz[0][0:TILES, 0:P], dots[:, n, :], ident[:, :],
                                        start=(n == 0), stop=(n == NH - 1))
            last.then_inc(lt_mm, 1)



def kernel(**inputs):
    import numpy as np
    import concourse.bacc as bacc
    from concourse.bass_utils import run_bass_kernel_spmd

    def get(name):
        return np.asarray(inputs[name])

    def cols(b):
        return np.ascontiguousarray(b.reshape(-1, P).T)

    def chunks(w):
        return w.reshape(-1, P, w.shape[1]).transpose(1, 0, 2).reshape(P, -1)

    w0 = get("L0_rec_top_w0")
    w0z = np.zeros((FC, KZ, H), w0.dtype)
    for f in range(1, NF):
        at = D + f * (f - 1) // 2
        c, k = f % FC, f // FC
        w0z[c, OFF[k]:OFF[k] + f, :] = w0[:, at:at + f].T
    idx = get("r_lS_i").reshape(TABLES, TILES, P).transpose(2, 1, 0).reshape(P, TILES * TABLES)
    arrays = {
        "idx": np.ascontiguousarray(idx),
        "bot_first": np.concatenate([get("r_dense_x").T, get("L0_rec_bot_w0").T], axis=1),
        "bot_biases": np.concatenate([cols(get(f"L0_rec_bot_b{i}")) for i in range(3)], axis=1),
        "bot_rest": np.concatenate([chunks(get(f"L0_rec_bot_w{i}").T) for i in (1, 2)], axis=1),
        "top_w0x_t": np.ascontiguousarray(w0[:, 0:D].T),
        "top_w0z_t": w0z,
        "top_b0": get("L0_rec_top_b0"),
        "top_w1_t": np.ascontiguousarray(get("L0_rec_top_w1").T),
        "top_b1": get("L0_rec_top_b1"),
        "top_w2": get("L0_rec_top_w2").reshape(-1),
        "top_b2": get("L0_rec_top_b2"),
        "emb": get("L0_rec_emb_W").reshape(TABLES * ROWS, D),
    }
    nc = bacc.Bacc("TRN2", target_bir_lowering=False, num_devices=1)
    args = {n: nc.dram_tensor(f"in_{n}", a.shape, mybir.dt.from_np(a.dtype), kind="ExternalInput").ap()
            for n, a in arrays.items()}
    out = nc.dram_tensor("out", (B, 1), F32, kind="ExternalOutput").ap()
    program(nc, out=out, **args)
    r = run_bass_kernel_spmd(nc, [{f"in_{n}": a for n, a in arrays.items()}], core_ids=[0])
    return r.results[0]["out"]
```

```python
from contextlib import ExitStack

import concourse.bass as bass
from concourse import mybir

F32 = mybir.dt.float32
F32R = mybir.dt.float32r
I32 = mybir.dt.int32
ACT = mybir.ActivationFunctionType
ALU = mybir.AluOpType

P = 128
B = 512
TILES = B // P
D = 128
TABLES = 26
ROWS = 12500
SLOTS = 32
NF = 1 + TABLES
S = P // SLOTS
G = P // S
PB = 4
ZBANKS = G // PB
NZ = S * TABLES
FC = 3
FK = NF // FC
COUNT = [FC * k + FC - 1 for k in range(FK)]
OFF = [sum(COUNT[:k]) for k in range(FK + 1)]
KZ = OFF[FK]
H = 1024
HC = H // P
N = 512
NH = H // N
DENSE, BOT0, BOT1 = 13, 512, 256
C0, C1 = BOT0 // P, BOT1 // P
GROUPS = [list(range(t, min(t + PB, TABLES))) for t in range(0, TABLES, PB)]
NG = len(GROUPS)
HALVES = [(0, 4), (4, NG)]
EA, ED = (NG + 1) // 2, NG // 2
ZA, ZD = ZBANKS // 2 + 1, ZBANKS // 2
L1_STEPS = [(a, w, c) for h in range(2) for a, w in (("hi", "hi"), ("hi", "lo"), ("lo", "hi"))
            for c in range(PB * h, PB * (h + 1))]
L1_HELD = {"z": 17, "ra": 18, "rb": 20}
L1_HELD_LAST = {"z": 14, "ra": 17, "rb": 20}
AMONG = {(0, 12): 2, (0, 18): 3, (1, 0): 4, (1, 6): 5, (1, 11): 6}
STAGES = 8
PIECES = [(c, n) for n in range(NH) for c in range(FC)] + [(FC + c, n) for n in range(NH) for c in range(HC)]


def program(nc, idx, bot_first, bot_biases, bot_rest, top_w0x_t, top_w0z_t, top_b0, top_w1_t, top_b1, top_w2, top_b2, emb, out):
    with ExitStack() as ctx:
        def sb(name, shape, dt=F32):
            return ctx.enter_context(nc.sbuf_tensor(name, shape, dt))

        def bank(name):
            return ctx.enter_context(nc.psum_tensor(name, [P, N], F32))

        def sem(name):
            return ctx.enter_context(nc.semaphore(name))

        idx_raw = sb("idx_raw", [P, TILES * TABLES], I32)
        idx_neg = sb("idx_neg", [P, TILES * TABLES], I32)
        idx_all = sb("idx_all", [P, TILES * TABLES], I32)
        idx_base = sb("idx_base", [P, TILES * TABLES], I32)
        idx_tile = sb("idx_tile", [P, TABLES], I32)
        ident = sb("ident", [P, P])
        bot_a = sb("bot_a", [DENSE, B + BOT0])
        dense_sb, bw0 = bot_a[:, 0:B], bot_a[:, B:B + BOT0]
        bot_b = sb("bot_b", [P, C0 + C1 + 1])
        bb0, bb1, bb2 = bot_b[:, 0:C0], bot_b[:, C0:C0 + C1], bot_b[:, C0 + C1:C0 + C1 + 1]
        bot_c = sb("bot_c", [P, C0 * BOT1 + C1 * D])
        bw1 = bot_c[:, 0:C0 * BOT1].rearrange("p (c n) -> p c n", n=BOT1)
        bw2 = bot_c[:, C0 * BOT1:].rearrange("p (c n) -> p c n", n=D)
        w0x = sb("w0x", [P, H])
        b1_all = sb("b1_all", [P, H])
        b1_parts = sb("b1_parts", [P, N], F32R)
        ones_f = sb("ones_f", [P, P])
        ones = sb("ones", [P, P], F32R)
        w2_row = sb("w2_row", [P, H])
        b2_col = sb("b2_col", [P, 1])
        stage = sb("stage", [P, STAGES, N])
        w_hi = sb("w_hi", [P, FC + HC, H], F32R)
        w_lo = sb("w_lo", [P, FC + HC, H], F32R)
        rows = sb("rows", [P, TABLES, D])
        vecs = sb("vecs", [P, G, S, SLOTS])
        x_t = sb("x_t", [P, B])
        xpart = sb("xpart", [P, TILES, H])
        zs = sb("zs", [P, NF, G])
        feat = sb("feat", [FC * G, S, KZ])
        r_hi = sb("r_hi", [KZ, FC, S, G], F32R)
        r_lo = sb("r_lo", [KZ, FC, S, G], F32R)
        h0 = sb("h0", [P, H])
        h0_hi = sb("h0_hi", [P, HC, P], F32R)
        h0_lo = sb("h0_lo", [P, HC, P], F32R)
        dots = sb("dots", [P, NH, TILES])
        probs = sb("probs", [TILES, P])
        bx0 = xpart[:, 0:2, :].rearrange("p a (b n) -> p (a b) n", n=B)
        bx1 = xpart[:, 2:3, :].rearrange("p a (b n) -> p (a b) n", n=B)
        b0_row = h0
        h1 = h0

        em = [bank(f"em{i}") for i in range(2)]
        zz = [bank(f"zz{i}") for i in range(2)]
        xx = [bank(f"xx{i}") for i in range(2)]
        mm = [bank(f"mm{i}") for i in range(2)]

        idx_in = sem("idx_in")
        bot0_in = sem("bot0_in")
        bot1_in = sem("bot1_in")
        bot2_in = sem("bot2_in")
        w0x_in = sem("w0x_in")
        last_in = sem("last_in")
        stage_in = [sem(f"stage_in{i}") for i in range(STAGES)]
        row_in = [sem(f"row_in{t}") for t in range(TABLES)]
        out_done = sem("out_done")
        const_step = sem("const_step")
        consts = sem("consts")
        idx_copied = sem("idx_copied")
        bot_mm = sem("bot_mm")
        xp_mm = sem("xp_mm")
        em_mm = sem("em_mm")
        z_mm = sem("z_mm")
        ra_mm = sem("ra_mm")
        rb_mm = sem("rb_mm")
        l0_mm = sem("l0_mm")
        h0_mm = sem("h0_mm")
        l1_mm = sem("l1_mm")
        lt_mm = sem("lt_mm")
        bot_act = sem("bot_act")
        w_hi_done = sem("w_hi_done")
        b1_hi_done = sem("b1_hi_done")
        em_act = sem("em_act")
        z_act = sem("z_act")
        ra_act = sem("ra_act")
        r_hi_done = sem("r_hi_done")
        h0_hi_done = sem("h0_hi_done")
        probs_done = sem("probs_done")
        idx_step = sem("idx_step")
        ones_set = sem("ones_set")
        zeroed = sem("zeroed")
        bot_dve = sem("bot_dve")
        w_lo_done = sem("w_lo_done")
        b1_lo_done = sem("b1_lo_done")
        em_dve = sem("em_dve")
        z_dve = sem("z_dve")
        ra_dve = sem("ra_dve")
        r_lo_done = sem("r_lo_done")
        h0_done = sem("h0_done")
        h0_lo_done = sem("h0_lo_done")
        mm_read = sem("mm_read")
        dots_done = sem("dots_done")

        def em_src(j):
            n = len(GROUPS[j])
            return em[j % 2][:, 0:n * P].rearrange("p (t s g) -> p t s g", s=S, g=G)

        def em_dst(j):
            a, n = 1 + GROUPS[j][0], len(GROUPS[j])
            return vecs[:, :, :, a:a + n].rearrange("p g s t -> p t s g")

        def x_src(k):
            return x_t[:, bass.ds(k * P, P)].rearrange("p (s g) -> p s g", g=G)

        def x_dst():
            return vecs[:, :, :, 0].rearrange("p g s -> p s g")

        z_banks = (*zz, *xx)
        ra_banks = (*zz, xx[0])
        rb_bank = xx[1]

        def xp_bank(i, n):
            return (xx, mm)[i % 2][n]

        def z_src(j, s):
            q = slice(s * SLOTS, (s + 1) * SLOTS)
            return z_banks[j % 4][q, 0:PB * NZ].rearrange("p (g s f) -> p s g f", s=S, f=TABLES)[:, s]

        def z_dst(j, s):
            q = slice(s * SLOTS, (s + 1) * SLOTS)
            return zs[q, 1:NF, j * PB:(j + 1) * PB].rearrange("p f g -> p g f")

        def ra_bank(k):
            return ra_banks[k // PB][0:FC * G, (k % PB) * P:(k % PB + 1) * P]

        def ra_src(k):
            return ra_bank(k).rearrange("p (s q) -> p s q", q=SLOTS)[:, :, 0:COUNT[k]]

        def rb_src():
            return rb_bank[0:KZ, 0:S * FC * G].rearrange("p (s c g) -> p c s g", c=FC, g=G)

        block = ctx.enter_context(nc.Block())

        @block.sync
        def _(sp):
            sp.dma_start(idx_raw[:, :], idx).then_inc(idx_in, 16)
            sp.dma_start(bot_a[:, :], bot_first).then_inc(bot0_in, 16)
            sp.dma_start(bot_c[:, :], bot_rest).then_inc(bot2_in, 16)
            sp.dma_start(bot_b[:, :], bot_biases).then_inc(bot1_in, 16)
            sp.dma_start(w0x[:, :], top_w0x_t).then_inc(w0x_in, 16)
            sp.dma_start(b0_row[:, :], top_b0.partition_broadcast(P)).then_inc(w0x_in, 16)
            for i, (c, n) in enumerate(PIECES):
                if i >= STAGES:
                    sp.wait_ge(w_lo_done, i - STAGES + 1)
                cols = slice(n * N, (n + 1) * N)
                if c < FC:
                    sp.dma_start(stage[0:KZ, i % STAGES, :], top_w0z_t[c, :, cols]).then_inc(stage_in[i % STAGES], 16)
                else:
                    sp.dma_start(stage[:, i % STAGES, :], top_w1_t[(c - FC) * P:(c - FC + 1) * P, cols])\
                        .then_inc(stage_in[i % STAGES], 16)
                if i == 13:
                    sp.dma_start(b1_all[:, :], top_b1.partition_broadcast(P)).then_inc(last_in, 16)
                    sp.dma_start(w2_row[:, :], top_w2.partition_broadcast(P)).then_inc(last_in, 16)
                    sp.dma_start(b2_col[:, :], top_b2.partition_broadcast(P)).then_inc(last_in, 16)
            sp.wait_ge(probs_done, 1)
            sp.dma_start(out.rearrange("(t p) o -> t (p o)", p=P), probs[:, :]).then_inc(out_done, 16)
            sp.wait_ge(out_done, 16)

        @block.gpsimd
        def _(gp):
            nc.gpsimd.iota(idx_base[:, :], [[0, TILES], [ROWS, TABLES]], base=0, channel_multiplier=0)\
                .then_inc(consts, 1)
            nc.gpsimd.memset(ident[:, :], 0.0).then_inc(const_step, 1)
            gp.wait_ge(const_step, 1)
            nc.gpsimd.affine_select(out=ident[:, :], in_=ident[:, :], compare_op=ALU.not_equal, fill=1.0,
                                    base=0, pattern=[[-1, P]], channel_multiplier=1).then_inc(consts, 1)

            def gather(t, index):
                nc.gpsimd.indirect_dma_start(rows[:, t, :], None, emb, bass.IndirectOffsetOnAxis(index, 0)).then_inc(row_in[t], 16)

            gp.wait_ge(idx_step, 3)
            for t in range(TABLES):
                gather(t, idx_all[:, t:t + 1])
            with gp.Fori(1, TILES) as k:
                for i, (g0, g1) in enumerate(HALVES):
                    t0, t1 = GROUPS[g0][0], GROUPS[g1 - 1][-1] + 1
                    gp.wait_ge(idx_copied, 2 * k + i - 1)
                    nc.gpsimd.nop(nofuse=True)
                    for t in range(t0, t1):
                        gather(t, idx_tile[:, t:t + 1])

        @block.scalar
        def _(act):
            def split_weights(first, end):
                for i in range(first, end):
                    c, n = PIECES[i]
                    kp = KZ if c < FC else P
                    act.wait_ge(stage_in[i % STAGES], 16 * (i // STAGES + 1))
                    nc.scalar.activation(w_hi[0:kp, c, n * N:(n + 1) * N], stage[0:kp, i % STAGES, :], ACT.Copy)\
                        .then_inc(w_hi_done, 1)

            def embeddings(k, j):
                act.wait_ge(em_mm, NG * k + j + 1)
                if j == 0:
                    nc.scalar.activation(x_dst(), x_src(k), ACT.Copy)
                nc.scalar.activation(em_dst(j), em_src(j), ACT.Copy).then_inc(em_act, 1)

            def relu_bias(dst, src, bias):
                nc.scalar.activation(dst, src, ACT.Relu, bias=bias).then_inc(bot_act, 1)

            act.wait_ge(ones_set, 1)
            nc.scalar.activation(ones[:, :], ones_f[:, :], ACT.Copy).then_inc(b1_hi_done, 1)
            act.wait_ge(bot1_in, 16)
            act.wait_ge(bot_mm, 1)
            relu_bias(bx0[:, 0, :], mm[0][:, :], bb0[:, 0:1])
            split_weights(0, 2)
            act.wait_ge(bot_mm, 3)
            relu_bias(bx0[:, 2, :], xx[0][:, :], bb0[:, 2:3])
            split_weights(2, 8)
            act.wait_ge(bot_mm, C0 + 1)
            relu_bias(bx1[:, 0, :], zz[0][:, :], bb1[:, 0:1])
            split_weights(8, 12)
            act.wait_ge(bot_mm, C0 + C1 + 1)
            relu_bias(x_t[:, :], mm[0][:, :], bb2[:, 0:1])
            act.wait_ge(bot_act, 4)
            embeddings(0, 0)
            embeddings(0, 2)
            split_weights(12, len(PIECES))
            embeddings(0, 4)
            embeddings(0, 6)
            act.wait_ge(last_in, 48)
            act.wait_ge(zeroed, 3)
            nc.scalar.activation(b1_parts[0:1, :], b1_all[0:1, H - N:], ACT.Copy).then_inc(b1_hi_done, 1)

            def front(k, more=True):
                for j in range(0, ZBANKS, 2):
                    act.wait_ge(z_mm, ZBANKS * k + j + 1)
                    for s in range(S):
                        last = nc.scalar.activation(z_dst(j, s), z_src(j, s), ACT.Copy)
                    last.then_inc(z_act, 1)
                act.wait_ge(z_mm, ZBANKS * (k + 1))
                for s in range(S // 2, S):
                    last = nc.scalar.activation(z_dst(ZBANKS - 1, s), z_src(ZBANKS - 1, s), ACT.Copy)
                last.then_inc(z_act, 1)
                if more:
                    embeddings(k + 1, 0)
                act.wait_ge(ra_mm, 3 * k + 2)
                for i in range(PB):
                    last = nc.scalar.activation(feat[:, :, OFF[i]:OFF[i + 1]], ra_src(i), ACT.Copy)
                last.then_inc(ra_act, 1)
                act.wait_ge(ra_mm, 3 * k + 3)
                nc.scalar.activation(feat[:, :, OFF[FK - 1]:KZ], ra_src(FK - 1), ACT.Copy).then_inc(ra_act, 1)
                act.wait_ge(rb_mm, k + 1)
                nc.scalar.activation(r_hi[:, :, :, :], rb_src(), ACT.Copy).then_inc(r_hi_done, 1)

            def back(k, more=True):
                for h in range(2):
                    act.wait_ge(h0_mm, 2 * k + h + 1)
                    nc.scalar.activation(h0_hi[:, PB * h:PB * (h + 1), :], xx[h][:, :], ACT.Relu)\
                        .then_inc(h0_hi_done, 1)
                if more:
                    for j in range(2, NG, 2):
                        embeddings(k + 1, j)

            front(0)
            with act.Fori(0, TILES - 2) as k:
                back(k)
                front(k + 1)
            back(TILES - 2)
            front(TILES - 1, more=False)
            back(TILES - 1, more=False)

            act.wait_ge(lt_mm, 1)
            nc.scalar.activation(probs[:, :], zz[0][0:TILES, 0:P], ACT.Sigmoid, bias=b2_col[0:TILES, 0:1])\
                .then_inc(probs_done, 1)

        @block.vector
        def _(dve):
            nc.vector.memset(ones_f[:, :], 1.0).then_inc(ones_set, 1)
            nc.vector.memset(zs[:, 0, :], 0.0).then_inc(zeroed, 1)
            nc.vector.memset(vecs[:, :, :, NF:SLOTS], 0.0).then_inc(zeroed, 1)
            nc.vector.memset(b1_parts[:, :].bitcast(F32), 0.0).then_inc(zeroed, 1)
            dve.wait_ge(idx_in, 16)
            nc.vector.tensor_scalar(idx_neg[:, :], idx_raw[:, :], 0, ROWS, ALU.is_lt, ALU.mult).then_inc(idx_step, 1)
            dve.wait_ge(idx_step, 1)
            nc.vector.scalar_tensor_tensor(idx_raw[:, :], idx_raw[:, :], -ROWS, idx_neg[:, :], ALU.max, ALU.add)\
                .then_inc(idx_step, 1)
            dve.wait_ge(consts, 1)
            dve.wait_ge(idx_step, 2)
            nc.vector.scalar_tensor_tensor(idx_all[:, :], idx_raw[:, :], ROWS - 1, idx_base[:, :], ALU.min, ALU.add)\
                .then_inc(idx_step, 1)

            def split_weights(first, end):
                for i in range(first, end):
                    c, n = PIECES[i]
                    kp = KZ if c < FC else P
                    cols = slice(n * N, (n + 1) * N)
                    dve.wait_ge(w_hi_done, i + 1)
                    nc.vector.tensor_tensor(w_lo[0:kp, c, cols], stage[0:kp, i % STAGES, :],
                                            w_hi[0:kp, c, cols].bitcast(F32), ALU.subtract).then_inc(w_lo_done, 1)

            def next_indices(k, half):
                g0, g1 = HALVES[half]
                t0, t1 = GROUPS[g0][0], GROUPS[g1 - 1][-1] + 1
                dve.wait_ge(em_mm, NG * k - NG + g1)
                nc.vector.tensor_copy(idx_tile[:, t0:t1], idx_all[:, bass.ds(k * TABLES + t0, t1 - t0)])\
                    .then_inc(idx_copied, 1)

            def embeddings(k, j):
                dve.wait_ge(em_mm, NG * k + j + 1)
                nc.vector.tensor_copy(em_dst(j), em_src(j)).then_inc(em_dve, 1)

            def relu_bias(dst, src, bias):
                nc.vector.tensor_scalar(dst, src, bias, 0.0, ALU.add, ALU.max).then_inc(bot_dve, 1)

            dve.wait_ge(bot1_in, 16)
            dve.wait_ge(bot_mm, 2)
            relu_bias(bx0[:, 1, :], mm[1][:, :], bb0[:, 1:2])
            split_weights(0, 2)
            dve.wait_ge(bot_mm, 4)
            relu_bias(bx0[:, 3, :], xx[1][:, :], bb0[:, 3:4])
            split_weights(2, 8)
            dve.wait_ge(bot_mm, C0 + C1)
            relu_bias(bx1[:, 1, :], zz[1][:, :], bb1[:, 1:2])
            dve.wait_ge(w0x_in, 32)

            def first_layer_x(i):
                for n in range(NH):
                    dve.wait_ge(xp_mm, NH * i + n + 1)
                    nc.vector.tensor_tensor(xpart[:, i, n * N:(n + 1) * N], xp_bank(i, n)[:, :],
                                            b0_row[:, n * N:(n + 1) * N], ALU.add).then_inc(mm_read, 1)

            split_weights(8, 10)
            embeddings(0, 1)
            first_layer_x(0)
            split_weights(10, 12)
            first_layer_x(1)
            split_weights(12, 14)
            next_indices(1, 0)
            embeddings(0, 3)
            first_layer_x(2)
            split_weights(14, 16)
            embeddings(0, 5)
            first_layer_x(3)
            split_weights(16, 17)

            def front(k, pieces=(), more=True):
                if more:
                    next_indices(k + 1, 1)
                for j in range(1, ZBANKS, 2):
                    dve.wait_ge(z_mm, ZBANKS * k + j + 1)
                    for s in range(S if j < ZBANKS - 1 else S // 2):
                        last = nc.vector.tensor_copy(z_dst(j, s), z_src(j, s))
                    last.then_inc(z_dve, 1)
                    for i in pieces[j // 2:j // 2 + 1]:
                        split_weights(i, i + 1)
                dve.wait_ge(ra_mm, 3 * k + 1)
                for i in range(PB, 2 * PB):
                    last = nc.vector.tensor_copy(feat[:, :, OFF[i]:OFF[i + 1]], ra_src(i))
                last.then_inc(ra_dve, 1)
                if more:
                    embeddings(k + 1, 1)
                dve.wait_ge(r_hi_done, k + 1)
                for c in range(FC):
                    last = nc.vector.tensor_tensor(r_lo[:, c], rb_src()[:, c], r_hi[:, c].bitcast(F32), ALU.subtract)
                last.then_inc(r_lo_done, 1)

            def dot(k, n, biased=False):
                cols = slice(n * N, (n + 1) * N)
                dve.wait_ge(l1_mm, NH * k + n + 1)
                if not biased:
                    nc.vector.tensor_tensor(h1[:, cols], mm[n][:, :], b1_all[:, cols], ALU.add).then_inc(mm_read, 1)
                    dve.wait_ge(mm_read, NH * (TILES + k) + n + 1)
                nc.vector.scalar_tensor_tensor(h1[:, cols], mm[n][:, :] if biased else h1[:, cols], 0.0,
                                               w2_row[:, cols], ALU.max, ALU.mult,
                                               accum_out=dots[:, n, bass.ds(k, 1)]).then_inc(dots_done, 1)

            def back(k, more=True, more_indices=True):
                for n in range(NH):
                    dve.wait_ge(l0_mm, NH * k + n + 1)
                    nc.vector.tensor_tensor(h0[:, n * N:(n + 1) * N], mm[n][:, :],
                                            xpart[:, bass.ds(k, 1), n * N:(n + 1) * N].rearrange("p a n -> p (a n)"),
                                            ALU.add).then_inc(h0_done, 1)
                for h in range(2):
                    dve.wait_ge(h0_hi_done, 2 * k + h + 1)
                    nc.vector.scalar_tensor_tensor(h0_lo[:, PB * h:PB * (h + 1), :], xx[h][:, :], 0.0,
                                                   h0_hi[:, PB * h:PB * (h + 1), :].bitcast(F32),
                                                   ALU.max, ALU.subtract).then_inc(h0_lo_done, 1)
                if more_indices and more:
                    next_indices(k + 2, 0)
                if more:
                    embeddings(k + 1, 3)
                dot(k, 0)
                if more:
                    embeddings(k + 1, 5)

            front(0, range(17, 20))
            split_weights(20, len(PIECES))
            dve.wait_ge(last_in, 48)
            dve.wait_ge(b1_hi_done, 2)
            nc.vector.tensor_tensor(b1_parts[32:33, :], b1_all[0:1, H - N:], b1_parts[0:1, :].bitcast(F32), ALU.subtract)\
                .then_inc(b1_lo_done, 1)
            dve.wait_ge(mm_read, NH * TILES)
            with dve.Fori(0, TILES - 2) as k:
                back(k)
                front(k + 1)
                dot(k, 1)
            back(TILES - 2, more_indices=False)
            front(TILES - 1, more=False)
            dot(TILES - 2, 1)
            back(TILES - 1, more=False)
            dot(TILES - 1, 1, biased=True)

        @block.tensor
        def _(pe):
            def embeddings(k, j, prior=True):
                for t in GROUPS[j]:
                    pe.wait_ge(row_in[t], 16 * k + 16)
                if (prior or j >= 2) and j % 2 == 0:
                    pe.wait_ge(em_act, EA * k + j // 2)
                elif prior or j >= 2:
                    pe.wait_ge(em_dve, ED * k + j // 2)
                for i, t in enumerate(GROUPS[j]):
                    last = nc.tensor.transpose(em[j % 2][:, i * P:(i + 1) * P], rows[:, t, :], ident[:, :])
                last.then_inc(em_mm, 1)

            def first_layer_x(i):
                for n in range(NH):
                    if i > 1:
                        pe.wait_ge(mm_read, NH * (i - 2) + n + 1)
                    nc.tensor.matmul(xp_bank(i, n)[:, :], x_t[:, i * P:(i + 1) * P], w0x[:, n * N:(n + 1) * N],
                                     start=True, stop=True).then_inc(xp_mm, 1)

            pe.wait_ge(bot0_in, 16)
            for m, b in enumerate((mm[0], mm[1], xx[0], xx[1])):
                nc.tensor.matmul(b[:, :], bw0[:, m * P:(m + 1) * P], dense_sb, start=True, stop=True)\
                    .then_inc(bot_mm, 1)
            pe.wait_ge(bot2_in, 16)
            for m in range(C1):
                for c in range(C0):
                    if m == 0:
                        pe.wait_ge((bot_act, bot_dve)[c % 2], c // 2 + 1)
                    last = nc.tensor.matmul(zz[m][:, :], bw1[:, c, m * P:(m + 1) * P], bx0[:, c, :],
                                            start=(c == 0), stop=(c == C0 - 1))
                last.then_inc(bot_mm, 1)
            pe.wait_ge(consts, 2)
            for c in range(C1):
                pe.wait_ge((bot_act, bot_dve)[c], 3)
                last = nc.tensor.matmul(mm[0][:, :], bw2[:, c, :], bx1[:, c, :], start=(c == 0), stop=(c == C1 - 1))
                if c == 0:
                    embeddings(0, 0, prior=False)
            last.then_inc(bot_mm, 1)
            embeddings(0, 1, prior=False)

            pe.wait_ge(bot_act, 4)
            pe.wait_ge(w0x_in, 32)
            for i in range(TILES):
                first_layer_x(i)
                if i + 2 < 5:
                    embeddings(0, i + 2)
            embeddings(0, 5)
            embeddings(0, 6)
            pe.wait_ge(zeroed, 3)
            pe.wait_ge(mm_read, NH * (TILES - 1))

            def transposes_h0(k, h):
                pe.wait_ge(h0_done, 2 * k + h + 1)
                for c in range(PB):
                    q = PB * h + c
                    last = nc.tensor.transpose(xx[h][:, c * P:(c + 1) * P], h0[:, q * P:(q + 1) * P], ident[:, :])
                last.then_inc(h0_mm, 1)

            def layer1(k, n, first, end, bias=False):
                cols = slice(n * N, (n + 1) * N)
                for i in range(first, end):
                    part, w_part, c = L1_STEPS[i]
                    if i == 0 and bias:
                        pe.wait_ge(b1_lo_done, 1)
                        nc.tensor.matmul(mm[n][:, :], ones[:, :], b1_parts[:, :], start=True, stop=False)
                    if n == 0 and w_part == "hi" and c % PB == 0:
                        pe.wait_ge(h0_hi_done if part == "hi" else h0_lo_done, 2 * k + c // PB + 1)
                    last = nc.tensor.matmul(mm[n][:, :], (h0_hi if part == "hi" else h0_lo)[:, c, :],
                                            (w_hi if w_part == "hi" else w_lo)[:, FC + c, cols],
                                            start=(i == 0 and not bias), stop=(i == len(L1_STEPS) - 1))
                if end == len(L1_STEPS):
                    last.then_inc(l1_mm, 1)

            def front(k, held=L1_HELD, more=True):
                pe.wait_ge(em_act, EA * (k + 1))
                pe.wait_ge(em_dve, ED * (k + 1))
                for j in range(ZBANKS):
                    if j >= 4:
                        pe.wait_ge((z_act, z_dve)[j % 2], (ZA, ZD)[j % 2] * k + j // 2 - 1)
                    for g in range(PB * j, PB * (j + 1)):
                        o = z_banks[j % 4][:, (g % PB) * NZ:(g % PB + 1) * NZ]
                        last = nc.tensor.matmul(o, vecs[:, g, :, :], vecs[:, g, :, 1:NF], start=True, stop=True)
                    last.then_inc(z_mm, 1)
                if more:
                    embeddings(k + 1, 0)
                if held:
                    layer1(k - 1, 1, held["z"], held["ra"])
                pe.wait_ge(z_act, ZA * (k + 1))
                pe.wait_ge(z_dve, ZD * (k + 1))
                for some in (range(PB, 2 * PB), range(PB), range(2 * PB, FK)):
                    for i in some:
                        last = nc.tensor.transpose(ra_bank(i), zs[:, FC * i:FC * (i + 1), :], ident[:, :])
                    last.then_inc(ra_mm, 1)
                if more:
                    embeddings(k + 1, 1)
                if held:
                    layer1(k - 1, 1, held["ra"], held["rb"])
                pe.wait_ge(ra_act, 2 * (k + 1))
                pe.wait_ge(ra_dve, k + 1)
                for s in range(S):
                    last = nc.tensor.transpose(rb_bank[0:KZ, s * FC * G:(s + 1) * FC * G], feat[:, s, :],
                                               ident[0:FC * G, 0:FC * G])
                last.then_inc(rb_mm, 1)
                if held:
                    layer1(k - 1, 1, held["rb"], len(L1_STEPS))

            def back(k, held=L1_HELD, more=True):
                for n in range(NH):
                    cols = slice(n * N, (n + 1) * N)
                    pe.wait_ge(w_lo_done, FC * (n + 1))
                    pe.wait_ge(mm_read, NH * (TILES + k) + n - 1)
                    if n == 0:
                        pe.wait_ge(r_hi_done, k + 1)
                    for a, (r, w) in enumerate(((r_hi, w_hi), (r_hi, w_lo), (r_lo, w_hi))):
                        if n == 0 and a == 2:
                            pe.wait_ge(r_lo_done, k + 1)
                        for c in range(FC):
                            if n == 1 and (a, c) == (1, 2):
                                transposes_h0(k, 0)
                            last = nc.tensor.matmul(mm[n][:, :], r[:, c, :, :], w[0:KZ, c, cols],
                                                    start=(a == 0 and c == 0), stop=(a == 2 and c == FC - 1))
                    last.then_inc(l0_mm, 1)
                pe.wait_ge(w_lo_done, NH * FC + HC)
                layer1(k, 0, 0, 2 * PB)
                transposes_h0(k, 1)
                at = 2 * PB
                for n in range(NH):
                    pe.wait_ge(w_lo_done, NH * FC + HC * (n + 1))
                    end = held["z"] if more and n == 1 else len(L1_STEPS)
                    for i in sorted(i for m, i in AMONG if m == n) if more else ():
                        layer1(k, n, at, i)
                        embeddings(k + 1, AMONG[n, i])
                        at = i
                    layer1(k, n, at, end, bias=(n == 1 and not more))
                    at = 0

            front(0, held=None)
            with pe.Fori(0, TILES - 2) as k:
                back(k)
                front(k + 1)
            back(TILES - 2, L1_HELD_LAST)
            front(TILES - 1, L1_HELD_LAST, more=False)
            back(TILES - 1, more=False)
            for n in range(NH):
                pe.wait_ge(dots_done, NH * (TILES - 1) + n + 1)
                last = nc.tensor.matmul(zz[0][0:TILES, 0:P], dots[:, n, :], ident[:, :],
                                        start=(n == 0), stop=(n == NH - 1))
            last.then_inc(lt_mm, 1)

def kernel(**inputs):
    import numpy as np
    import concourse.bacc as bacc
    from concourse.bass_utils import run_bass_kernel_spmd

    def get(name):
        return np.asarray(inputs[name])

    def cols(b):
        return np.ascontiguousarray(b.reshape(-1, P).T)

    def chunks(w):
        return w.reshape(-1, P, w.shape[1]).transpose(1, 0, 2).reshape(P, -1)

    w0 = get("L0_rec_top_w0")
    w0z = np.zeros((FC, KZ, H), w0.dtype)
    for f in range(1, NF):
        at = D + f * (f - 1) // 2
        c, k = f % FC, f // FC
        w0z[c, OFF[k]:OFF[k] + f, :] = w0[:, at:at + f].T
    idx = get("r_lS_i").reshape(TABLES, TILES, P).transpose(2, 1, 0).reshape(P, TILES * TABLES)
    arrays = {
        "idx": np.ascontiguousarray(idx),
        "bot_first": np.concatenate([get("r_dense_x").T, get("L0_rec_bot_w0").T], axis=1),
        "bot_biases": np.concatenate([cols(get(f"L0_rec_bot_b{i}")) for i in range(3)], axis=1),
        "bot_rest": np.concatenate([chunks(get(f"L0_rec_bot_w{i}").T) for i in (1, 2)], axis=1),
        "top_w0x_t": np.ascontiguousarray(w0[:, 0:D].T),
        "top_w0z_t": w0z,
        "top_b0": get("L0_rec_top_b0"),
        "top_w1_t": np.ascontiguousarray(get("L0_rec_top_w1").T),
        "top_b1": get("L0_rec_top_b1"),
        "top_w2": get("L0_rec_top_w2").reshape(-1),
        "top_b2": get("L0_rec_top_b2"),
        "emb": get("L0_rec_emb_W").reshape(TABLES * ROWS, D),
    }
    nc = bacc.Bacc("TRN2", target_bir_lowering=False, num_devices=1)
    args = {n: nc.dram_tensor(f"in_{n}", a.shape, mybir.dt.from_np(a.dtype), kind="ExternalInput").ap()
            for n, a in arrays.items()}
    out = nc.dram_tensor("out", (B, 1), F32, kind="ExternalOutput").ap()
    program(nc, out=out, **args)
    r = run_bass_kernel_spmd(nc, [{f"in_{n}": a for n, a in arrays.items()}], core_ids=[0])
    return r.results[0]["out"]
```
